# Optimizing a Trainium2 kernel written in Bass

```python
import numpy as np
import jax
import jax.numpy as jnp

def _softmax(x, axis=-1):
    return jax.nn.softmax(x, axis=axis)

def _gelu(x):
    return jax.nn.gelu(x, approximate=True)

def _silu(x):
    return jax.nn.silu(x)

def _sigmoid(x):
    return jax.nn.sigmoid(x)

def _layernorm(x, axis=-1, eps=1e-05):
    m = jnp.mean(x, axis=axis, keepdims=True)
    v = jnp.var(x, axis=axis, keepdims=True)
    return (x - m) / jnp.sqrt(v + eps)

def _scatter_add(tgt, idx, src, axis=0):
    return tgt.at[idx].add(src)

def _segment_sum(src, seg, n):
    return jax.ops.segment_sum(src, seg, n)
kernel_name = 'mk_flamingo_gated_d1_seqx_r2_70709e'

def setup_inputs(seed: int=0):
    np.random.seed(seed)
    _w = jnp.asarray

    def _rec_inputs():
        import jax
        import jax.numpy as jnp
        _rk = jax.random.key(seed)
        x = -0.000125 + 0.9999 * jax.random.normal(jax.random.fold_in(_rk, 1), (2, 1024, 2048), jnp.float32)
        _lenS = 1024 - jax.random.randint(jax.random.fold_in(_rk, 7), (2,), 0, max(1, 1024 // 4) + 1, jnp.int32)
        _lenS2 = 2048 - jax.random.randint(jax.random.fold_in(_rk, 8), (2,), 0, max(1, 2048 // 4) + 1, jnp.int32)
        _ctx_4096P = jax.random.normal(jax.random.fold_in(_rk, 11), (2, 16, 2048), jnp.float32)
        _ctx_4096c = jax.random.dirichlet(jax.random.fold_in(_rk, 511), 0.3 * jnp.ones((16,), jnp.float32), (2, 2048))
        _ctx_4096t = jnp.einsum('bsk,bkd->bsd', _ctx_4096c, _ctx_4096P)
        _ctx_4096t = _ctx_4096t * jax.lax.rsqrt(jnp.mean(jnp.square(_ctx_4096t)) + 1e-12) * 0.953939
        ctx_4096 = -5.72187e-05 + 0.999849 * (_ctx_4096t + 0.3 * jax.random.normal(jax.random.fold_in(_rk, 611), (2, 2048, 2048), jnp.float32))
        _g = jax.random.normal(jax.random.fold_in(_rk, 9001), (2, 1), jnp.float32)
        _g = jnp.sign(_g) * jnp.maximum(jnp.abs(_g), 1.0) + (_g == 0) * 1.0
        g_xattn = _g[0]
        g_ffn = _g[1]
        return (x, ctx_4096, g_xattn, g_ffn)
    x, ctx_4096, g_xattn, g_ffn = _rec_inputs()

    def _L0_xattn_setup():
        import jax, jax.numpy as jnp
        import numpy as np
        QMIN = 0.0
        QMAX = 255.0

        def fake_quant(x, scale, zp):
            s = scale.reshape(())
            z = zp.reshape(())
            q = jnp.clip(jnp.round(x / s + z), QMIN, QMAX)
            return (q - z) * s
        key = jax.random.key(seed)
        k1, k2 = jax.random.split(key)
        B, M, K, N = (4, 1024, 2048, 2048)
        x1 = jax.random.normal(k1, (B, M, K), dtype=jnp.float32)
        x2 = jax.random.normal(k2, (B, K, N), dtype=jnp.float32)
        x1_scale = jnp.full((1,), 8.0 / 255.0, dtype=jnp.float32)
        x1_zp = jnp.full((1,), 128.0, dtype=jnp.float32)
        x2_scale = jnp.full((1,), 8.0 / 255.0, dtype=jnp.float32)
        x2_zp = jnp.full((1,), 128.0, dtype=jnp.float32)
        return {'x1': x1, 'x2': x2, 'x1_scale': x1_scale, 'x1_zp': x1_zp, 'x2_scale': x2_scale, 'x2_zp': x2_zp}
    _L0_xattn_all = _L0_xattn_setup()
    _L0_xattn_in = {k: v for k, v in _L0_xattn_all.items() if k in ('x1_scale', 'x1_zp', 'x2_scale', 'x2_zp')}
    del _L0_xattn_all

    def _L0_ffn_setup():
        import jax, jax.numpy as jnp
        import numpy as np
        LORA_R = 16
        SCALE = 16.0 / np.sqrt(16.0)
        NUM_EXPERTS = 4
        TOP_K = 2
        IN_F = 2048
        OUT_F = 2048
        key = jax.random.key(seed)
        k_x, k_a, k_b, k_r = jax.random.split(key, 4)
        x = jax.random.normal(k_x, (2, 1024, IN_F), dtype=jnp.float32)
        A = jax.random.normal(k_a, (NUM_EXPERTS, LORA_R, IN_F), dtype=jnp.float32) * (1.0 / np.sqrt(IN_F))
        B = jax.random.normal(k_b, (NUM_EXPERTS, OUT_F, LORA_R), dtype=jnp.float32) * 0.02
        Wr = jax.random.normal(k_r, (NUM_EXPERTS, IN_F), dtype=jnp.float32) * 0.02
        return {'x': x, 'A': A, 'B': B, 'Wr': Wr}
    _L0_ffn_all = _L0_ffn_setup()
    _L0_ffn_in = {k: v for k, v in _L0_ffn_all.items() if k in ('A', 'B', 'Wr')}
    del _L0_ffn_all
    return {'x': x, 'ctx_4096': ctx_4096, 'g_xattn': g_xattn, 'g_ffn': g_ffn, 'L0_xattn_x1_scale': _L0_xattn_in['x1_scale'], 'L0_xattn_x1_zp': _L0_xattn_in['x1_zp'], 'L0_xattn_x2_scale': _L0_xattn_in['x2_scale'], 'L0_xattn_x2_zp': _L0_xattn_in['x2_zp'], 'L0_ffn_A': _L0_ffn_in['A'], 'L0_ffn_B': _L0_ffn_in['B'], 'L0_ffn_Wr': _L0_ffn_in['Wr']}

def reference(x, ctx_4096, g_xattn, g_ffn, L0_xattn_x1_scale, L0_xattn_x1_zp, L0_xattn_x2_scale, L0_xattn_x2_zp, L0_ffn_A, L0_ffn_B, L0_ffn_Wr):
    import jax
    import jax.numpy as jnp

    def _L0_xattn_ref(x1, x2, x1_scale, x1_zp, x2_scale, x2_zp):
        import jax, jax.numpy as jnp
        import numpy as np
        QMIN = 0.0
        QMAX = 255.0

        def fake_quant(x, scale, zp):
            s = scale.reshape(())
            z = zp.reshape(())
            q = jnp.clip(jnp.round(x / s + z), QMIN, QMAX)
            return (q - z) * s
        q1 = fake_quant(x1, x1_scale, x1_zp)
        q2 = fake_quant(x2, x2_scale, x2_zp)
        return jnp.matmul(q1, q2)

    def _L0_ffn_ref(x, A, B, Wr):
        import jax, jax.numpy as jnp
        import numpy as np
        LORA_R = 16
        SCALE = 16.0 / np.sqrt(16.0)
        NUM_EXPERTS = 4
        TOP_K = 2
        IN_F = 2048
        OUT_F = 2048
        orig_shape = x.shape
        flat = x.reshape(-1, orig_shape[-1])
        logits = flat @ Wr.T
        topk_vals, topk_idx = jax.lax.top_k(logits, TOP_K)
        T = flat.shape[0]
        neg_inf = jnp.finfo(logits.dtype).min
        sparse = jnp.full_like(logits, neg_inf)
        rows = jnp.arange(T)[:, None]
        sparse = sparse.at[rows, topk_idx].set(topk_vals)
        gates = jax.nn.softmax(sparse, axis=-1)
        mid = jnp.einsum('tf,erf->ter', flat, A)
        all_deltas = jnp.einsum('ter,eor->teo', mid, B) * SCALE
        delta = jnp.sum(gates[:, :, None] * all_deltas, axis=1)
        return delta.reshape(*orig_shape[:-1], -1)
    x = x + jnp.tanh(g_xattn[0]) * _L0_xattn_ref(_layernorm(x, axis=-1), ctx_4096, L0_xattn_x1_scale, L0_xattn_x1_zp, L0_xattn_x2_scale, L0_xattn_x2_zp)
    x = x + jnp.tanh(g_ffn[0]) * _L0_ffn_ref(_layernorm(x, axis=-1), L0_ffn_A, L0_ffn_B, L0_ffn_Wr)
    return x

_drawn_inputs = setup_inputs


def setup_inputs(seed=0):
    import zlib

    import numpy as np

    out = dict(_drawn_inputs(seed))
    spreads = {}
    factors = {'L0_ffn_A': 7.429, 'L0_ffn_B': 7.56, 'L0_ffn_Wr': 8.0}
    for name, (base, spread) in spreads.items():
        noise = np.random.default_rng([zlib.crc32(name.encode()), seed]).standard_normal(out[name].shape)
        drawn = base * np.exp(spread * noise) if base else spread * noise
        out[name] = jnp.asarray(drawn.astype(out[name].dtype))
    for name, factor in factors.items():
        out[name] = (out[name] * factor).astype(out[name].dtype)
    return out
```

```python
from contextlib import ExitStack

import concourse.bass as bass
import concourse.mybir as mybir

ALU = mybir.AluOpType
ACT = mybir.ActivationFunctionType
AX = mybir.AxisListType
F32 = mybir.dt.float32
F32R = mybir.dt.float32r
BF16 = mybir.dt.bfloat16
F16 = mybir.dt.float16
I32 = mybir.dt.int32

P = 128
BANK = 512
HALF = 1024
ROUND = 1.5 * 2.0 ** 23
QMAX = 255.0
EPS = 1e-5
LORA_SCALE = 4.0
STAGES = 4


def build(nc, x, ctx_in, g_xattn, g_ffn, s1, z1, s2, z2, lora_a, lora_b, router, out):
    B, M, D = x.shape
    K, N = ctx_in.shape[1:]
    E, R, _ = lora_a.shape
    ER = E * R
    J = ER + E
    KT, NB = K // P, N // BANK
    TILES = B * M // P
    PER_B = M // P
    HALVES = 2 * KT
    Q = HALVES // PER_B
    HK = HALF // P
    assert (D, N, Q, NB, 2 * ER) == (2 * HALF, D, STAGES, 4, P)

    x_rows = x.rearrange("b m d -> (b m) d")
    out_rows = out.rearrange("b m d -> (b m) d")
    ctx_rows = ctx_in.rearrange("b k n -> (b k) n")

    with ExitStack() as stack:
        def sb(name, shape, dt):
            return stack.enter_context(nc.sbuf_tensor(name, shape, dt))

        def sem(name):
            return stack.enter_context(nc.semaphore(name))

        q2 = sb("q2", [P, B, KT, N], F16)
        ctx_stage = sb("ctx_stage", [P, STAGES, HALF], F32)
        xt = sb("xt", [P, 2, D], F32)
        x1 = sb("x1", [P, 2, D], F32)
        q1T = sb("q1T", [P, 2, KT, P], F16)
        lora_bT = sb("lora_bT", [P, N], F32R)
        a_parts = sb("a_parts", [P, KT, 3, J], BF16)
        w1 = sb("w1", [P, HALF], F32)
        q1 = sb("q1", [P, HALF], F16)
        h2 = sb("h2", [P, HALF], F32)
        h_hi = sb("h_hi", [P, 2, HALF], F16)
        h_lo = sb("h_lo", [P, 2, HALF], F16)
        hT = sb("hT", [P, 2, HK, P], F16)
        ident_h = sb("ident_h", [P, P], F16)
        ident_f = sb("ident_f", [P, P], F32)
        small_tile = sb("small_tile", [P, 176], F32)
        used = [0]

        def small(*dims):
            n, first = 1, used[0]
            for d in dims:
                n *= d
            used[0] += n
            assert used[0] <= 176
            view = small_tile[:, first:first + n]
            if len(dims) == 2:
                return view.rearrange("p (a b) -> p a b", b=dims[1])
            if len(dims) == 3:
                return view.rearrange("p (a b c) -> p a b c", b=dims[1], c=dims[2])
            return view

        par = small(6)
        inv_s = small(2)
        centre = small(2)
        neg_centre = small(2)
        rest = small(2)
        rest_part = sb("rest_part", [P, 3, 2], BF16)
        rest_tmp = small(2)
        rest_flag = small(2)
        rest_any = sb("rest_any", [P, 1], I32)
        gates_raw = small(2)
        gain = small(2)
        half_neg = small(1)
        x_stats = small(NB, 6)
        x_mv = small(2)
        x_var = small(1)
        x_rstd = small(1)
        q_scale = small(2)
        q_neg = small(1)
        h_stats = small(NB, 6)
        h_mv = small(2)
        h_var = small(1)
        h_rstd = small(1)
        h_bias = small(1)
        before = small(E, E)
        mids = sb("mids", [P, J], F32)
        beats = small(E, 2, E)
        rank = small(E)
        top = small(1)
        shifted = small(E)
        expd = small(E)
        kept = small(E)
        kept_sum = small(1)
        kept_inv = small(1)
        gate = small(E)
        gated = sb("gated", [P, 2, E, R], F32)
        gT_hi = sb("gT_hi", [P, P], F32R)
        gT_lo = sb("gT_lo", [P, P], F32R)

        def bank(name):
            return stack.enter_context(nc.psum_tensor(name, [P, BANK], F32))

        ps_main = [bank("ps_main0"), bank("ps_main1")]
        ps_turn = [bank("ps_turn0"), bank("ps_turn1")]
        ps_mid = bank("ps_mid")
        ps_gate = bank("ps_gate")
        ps_delta = [bank("ps_delta0"), bank("ps_delta1")]
        ps_first = ps_main + ps_delta
        ps_small = [ps_mid, ps_gate]

        par_loaded, a_loaded, b_loaded = sem("par_loaded"), sem("a_loaded"), sem("b_loaded")
        x_loaded = [sem("x_loaded0"), sem("x_loaded1")]
        ctx_loaded = [sem(f"ctx_loaded{q}") for q in range(STAGES)]
        out_stored = [sem(f"out_stored{n}") for n in range(NB)]
        ident_zero, ident_ready, masks_ready = sem("ident_zero"), sem("ident_ready"), sem("masks_ready")
        par_step, consts_ready, tanh_done = sem("par_step"), sem("consts_ready"), sem("tanh_done")
        weights_turned, weights_split = sem("weights_turned"), sem("weights_split")
        a_step, b_spread, b_step = sem("a_step"), sem("b_spread"), sem("b_step")
        ctx_scaled, ctx_rounded = sem("ctx_scaled"), sem("ctx_rounded")
        ctx_even, ctx_odd = sem("ctx_even"), sem("ctx_odd")
        ctx2_coded = sem("ctx2_coded")
        x_stat_step, x_var_ready, x_rstd_ready = sem("x_stat_step"), sem("x_var_ready"), sem("x_rstd_ready")
        q_step, q_scale_ready = sem("q_step"), sem("q_scale_ready")
        x_scaled, x_rounded, x_coded = sem("x_scaled"), sem("x_rounded"), sem("x_coded")
        q1_turned, q1T_ready = sem("q1_turned"), sem("q1T_ready")
        main_done, x1_ready = sem("main_done"), sem("x1_ready")
        h_stat_step, h_var_ready, h_rstd_ready = sem("h_stat_step"), sem("h_var_ready"), sem("h_rstd_ready")
        h_bias_ready = sem("h_bias_ready")
        h2_ready, h_hi_ready, h_lo_ready = sem("h2_ready"), sem("h_hi_ready"), sem("h_lo_ready")
        hi_turned, hiT_ready = sem("hi_turned"), sem("hiT_ready")
        lo_turned, loT_ready = sem("lo_turned"), sem("loT_ready")
        hi_used, lo_used, mid_done, mids_read = sem("hi_used"), sem("lo_used"), sem("mid_done"), sem("mids_read")
        gate_step, shifted_ready, exp_done = sem("gate_step"), sem("shifted_ready"), sem("exp_done")
        gated_ready, gate_turned, gT_step, gT_ready = sem("gated_ready"), sem("gate_turned"), sem("gT_step"), sem("gT_ready")
        pool_waited, dve_waited = sem("pool_waited"), sem("dve_waited")
        delta_done, out_ready = sem("delta_done"), sem("out_ready")

        block = stack.enter_context(nc.Block())

        def upto(b, i, per, extra):
            return per * b + extra + (i * (2 * per) if not isinstance(i, int) else 0)

        def wait(eng, s, b, i, per, extra):
            if isinstance(i, int) and per * b + extra <= 0:
                return
            eng.wait_ge(s, upto(b, i, per, extra))

        def wait_half(eng, s, b, i, n, unit=16):
            eng.wait_ge(s, unit * (b // 2 + n) + (i * unit if not isinstance(i, int) else 0))

        def slots(eng, body):
            for b in range(3):
                body(b, 0)
            with eng.Fori(0, (PER_B - 4) // 2) as i:
                body(3, i)
                body(4, i)
            body(PER_B - 1, 0)
            with eng.Fori(0, (PER_B - 2) // 2) as i:
                body(PER_B, i)
                body(PER_B + 1, i)
            body(TILES - 2, 0)
            body(TILES - 1, 0)

        def batch(b):
            return 0 if b < PER_B else 1

        def cols(n):
            return slice(n * BANK, (n + 1) * BANK)

        def half(h):
            return slice(h * HALF, (h + 1) * HALF)

        def as16(ps, dt):
            return ps[:, :].bitcast(dt)

        a_raw = x1[:, 0, :]
        b_raw = x1[:, 1, 0:HALF].rearrange("p (e c r) -> p e c r", e=E, r=R)
        b_twice = x1[:, 1, HALF:D].rearrange("p (c d e r) -> p c d e r", d=2, e=E, r=R)
        b_flat = x1[:, 1, HALF:D].rearrange("p (c j) -> p c j", j=P)
        b_cols = lora_bT[:, :].rearrange("q (p c) -> q c p", c=KT)
        NC8 = HALF // P

        @block.sync
        def _(sp):
            def load_x(b, i):
                if b >= 2:
                    wait(sp, x1_ready, b, i, NB, -NB)
                rows = bass.ts(b, P) if isinstance(i, int) else bass.ts(i * 2 + b, P)
                sp.dma_start(xt[:, b % 2, :], x_rows[rows, :]).then_inc(x_loaded[b % 2], 16)

            def load_ctx(row, h, q):
                sp.dma_start(ctx_stage[:, q, :], ctx_rows[row, half(h)]).then_inc(ctx_loaded[q], 16)

            load_x(0, 0)
            for n, v in enumerate((s1, s2, z1, z2, g_xattn, g_ffn)):
                sp.dma_start(par[:, n:n + 1], v.unsqueeze(0).to_broadcast([P, 1])).then_inc(par_loaded, 16)
            for j in range(HALVES + Q):
                if j >= STAGES:
                    sp.wait_ge(ctx_even if j % 2 == 0 else ctx_odd, (j - STAGES) // 2 + 1)
                load_ctx(bass.ts(j // 2, P), j % 2, j % STAGES)
                if j == 3:
                    sp.dma_start(a_raw[0:ER, :], lora_a.rearrange("e r f -> (e r) f")).then_inc(a_loaded, 16)
                    sp.dma_start(a_raw[ER:J, :], router).then_inc(a_loaded, 16)
                    sp.dma_start(x1[:, 1, 0:HALF].rearrange("p (e c) -> p e c", e=E),
                                 lora_b.rearrange("e (p c) r -> p e (c r)", c=KT)).then_inc(b_loaded, 16)
                if j == 7:
                    load_x(1, 0)

            def slot(b, i):
                if 1 <= b < TILES - 1:
                    load_x(b + 1, i)
                if b >= 2:
                    store_out(b - 2, i, (2, 3))
                if b < PER_B - 1:
                    for q in range(Q):
                        wait(sp, ctx2_coded, b, i, Q, q + 1)
                        row = (HALVES + Q * (b + 1) + q) // 2
                        rows = bass.ts(row, P) if isinstance(i, int) else bass.ts(i * Q + row, P)
                        load_ctx(rows, q % 2, q)
                if b >= 1:
                    store_out(b - 1, i, (0, 1))

            def store_out(b, i, banks):
                rows = bass.ts(b, P) if isinstance(i, int) else bass.ts(i * 2 + b, P)
                for n in banks:
                    wait(sp, out_ready, b, i, NB, n + 1)
                    sp.dma_start(out_rows[rows, cols(n)], x1[:, b % 2, cols(n)]).then_inc(out_stored[n], 16)

            slots(sp, slot)
            store_out(TILES - 2, 0, (2, 3))
            store_out(TILES - 1, 0, range(NB))
            for n in range(NB):
                sp.wait_ge(out_stored[n], 16 * TILES)

        @block.gpsimd
        def _(pool):
            nc.gpsimd.memset(ident_h[:, :], 0.0).then_inc(ident_zero, 1)
            nc.gpsimd.memset(ident_f[:, :], 0.0).then_inc(ident_zero, 1)
            nc.gpsimd.memset(before[:, :, :], 1.0).then_inc(ident_zero, 1)
            nc.gpsimd.memset(half_neg[:, :], -0.5).then_inc(masks_ready, 1)
            pool.wait_ge(ident_zero, 3)
            for m in (ident_h, ident_f):
                nc.gpsimd.affine_select(out=m[:, :], in_=m[:, :], compare_op=ALU.not_equal, fill=1.0, base=0,
                                        pattern=[[-1, P]], channel_multiplier=1).then_inc(ident_ready, 1)
            nc.gpsimd.affine_select(out=before[:, :, :], in_=before[:, :, :], compare_op=ALU.is_gt, fill=0.0, base=0,
                                    pattern=[[1, E], [-1, E]], channel_multiplier=0).then_inc(masks_ready, 1)
            pool.wait_ge(masks_ready, 2)
            pool.wait_ge(consts_ready, 1)

            def power_x(b, i):
                wait(pool, x_var_ready, b, i, 1, 1)
                nc.gpsimd.tensor_tensor(x_rstd[:, :], x_var[:, :], half_neg[:, :], ALU.pow).then_inc(x_rstd_ready, 1)

            def power_h(b, i):
                wait(pool, h_var_ready, b, i, 1, 1)
                nc.gpsimd.tensor_tensor(h_rstd[:, :], h_var[:, :], half_neg[:, :], ALU.pow).then_inc(h_rstd_ready, 1)

            def code_x(b, i, h):
                wait(pool, x_rounded, b, i, 2, h + 1)
                wait(pool, q1_turned, b, i, 2, h)
                pool.sem_inc(pool_waited, 1)
                nc.gpsimd.tensor_scalar(q1[:, :], w1[:, :], neg_centre[:, 0:1], 1.0, ALU.add, ALU.mult).then_inc(x_coded, 1)

            def low_part(b, i, h):
                wait(pool, h2_ready, b, i, 2, h + 1)
                wait(pool, h_hi_ready, b, i, 2, h + 1)
                wait(pool, lo_turned, b, i, 2, h - 1)
                nc.gpsimd.tensor_tensor(h_lo[:, h, :], h2[:, :], h_hi[:, h, :], ALU.subtract).then_inc(h_lo_ready, 1)

            power_x(0, 0)
            for j in range(1, HALVES, 2):
                pool.wait_ge(ctx_rounded, j + 1)
                nc.gpsimd.tensor_scalar(q2[:, 0, j // 2, half(1)], ctx_stage[:, j % STAGES, :], neg_centre[:, 1:2], 1.0,
                                        ALU.add, ALU.mult).then_inc(ctx_odd, 1)
                if j in (1, 5):
                    code_x(0, 0, j // 4)
                if j == 13:
                    power_x(1, 0)
                if j in (17, 21):
                    code_x(1, 0, (j - 17) // 4)

            def slot(b, i):
                if b >= 1:
                    low_part(b - 1, i, 0)
                    low_part(b - 1, i, 1)
                if 1 <= b < TILES - 1:
                    power_x(b + 1, i)
                    code_x(b + 1, i, 0)
                    code_x(b + 1, i, 1)
                power_h(b, i)

            slots(pool, slot)
            for h in range(2):
                low_part(TILES - 1, 0, h)

        @block.scalar
        def _(act):
            act.wait_ge(par_loaded, 96)
            nc.scalar.activation(gates_raw[:, :], par[:, 4:6], ACT.Tanh).then_inc(tanh_done, 1)
            act.wait_ge(consts_ready, 1)

            def scale_ctx(b, i, q, n):
                wait(act, ctx_loaded[q], b, i, 16, 16 * n)
                nc.scalar.activation(ctx_stage[:, q, :], ctx_stage[:, q, :], ACT.Relu,
                                     bias=par[:, 3:4], scale=inv_s[:, 1:2]).then_inc(ctx_scaled, 1)

            def scale_x(b, i, h):
                wait(act, q_scale_ready, b, i, 1, 1)
                wait(act, x_coded, b, i, 2, h)
                nc.scalar.activation(w1[:, :], xt[:, b % 2, half(h)], ACT.Relu,
                                     bias=q_scale[:, 1:2], scale=q_scale[:, 0:1]).then_inc(x_scaled, 1)

            def copy_q1T(b, i, h):
                wait(act, q1_turned, b, i, 2, h + 1)
                nc.scalar.copy(q1T[:, b % 2, h * HK:(h + 1) * HK, :],
                               as16(ps_turn[h], F16).rearrange("p (k m) -> p k m", m=P)).then_inc(q1T_ready, 1)

            def high_part(b, i, h):
                wait(act, h_bias_ready, b, i, 1, 1)
                wait(act, hi_turned, b, i, 2, h - 1)
                nc.scalar.activation(h_hi[:, h, :], x1[:, b % 2, half(h)], ACT.Identity,
                                     bias=h_bias[:, :], scale=h_rstd[:, :]).then_inc(h_hi_ready, 1)

            def normal_half(b, i, h):
                wait(act, h_lo_ready, b, i, 2, h)
                nc.scalar.activation(h2[:, :], x1[:, b % 2, half(h)], ACT.Identity,
                                     bias=h_bias[:, :], scale=h_rstd[:, :]).then_inc(h2_ready, 1)

            def copy_hiT(b, i, h):
                wait(act, hi_turned, b, i, 2, h + 1)
                wait(act, lo_used, b, i, 2, h - 1)
                nc.scalar.copy(hT[:, h, :, :],
                               as16(ps_turn[h], F16).rearrange("p (k m) -> p k m", m=P)).then_inc(hiT_ready, 1)

            def gate_exp(b, i):
                wait(act, shifted_ready, b, i, 1, 1)
                nc.scalar.activation(expd[:, :], shifted[:, :], ACT.Exp).then_inc(exp_done, 1)

            for j in range(HALVES):
                scale_ctx(0, 0, j % STAGES, j // STAGES + 1)
                if j in (0, 3):
                    scale_x(0, 0, j // 3)
                if j in (8, 9):
                    copy_q1T(0, 0, j - 8)
                if j in (16, 19):
                    scale_x(1, 0, (j - 16) // 3)
                if j in (26, 27):
                    copy_q1T(1, 0, j - 26)

            def slot(b, i):
                def ctx_half(q):
                    if b < PER_B:
                        scale_ctx(b, i, q, HALVES // STAGES + 1)
                if b >= 1:
                    high_part(b - 1, i, 0)
                    normal_half(b - 1, i, 0)
                    high_part(b - 1, i, 1)
                ctx_half(0)
                ctx_half(1)
                if b >= 1:
                    normal_half(b - 1, i, 1)
                    copy_hiT(b - 1, i, 0)
                    copy_hiT(b - 1, i, 1)
                ahead = 1 <= b < TILES - 1
                for h in range(2):
                    if ahead:
                        scale_x(b + 1, i, h)
                    ctx_half(2 + h)
                if ahead:
                    copy_q1T(b + 1, i, 0)
                if b >= 1:
                    gate_exp(b - 1, i)
                if ahead:
                    copy_q1T(b + 1, i, 1)

            slots(act, slot)
            t = TILES - 1
            high_part(t, 0, 0)
            normal_half(t, 0, 0)
            high_part(t, 0, 1)
            normal_half(t, 0, 1)
            copy_hiT(t, 0, 0)
            copy_hiT(t, 0, 1)
            gate_exp(t, 0)

        @block.tensor
        def _(pe):
            flag = pe.alloc_register("rest_flag_reg")

            pe.wait_ge(consts_ready, 1)
            pe.reg_load(flag, rest_any[0:1, 0:1])

            def turn_q1(b, i, h):
                wait(pe, x_coded, b, i, 2, h + 1)
                wait(pe, loT_ready, b, i, 2, h - 3)
                for k in range(HK):
                    mm = pe.transpose(as16(ps_turn[h], F16)[:, k * P:(k + 1) * P], q1[:, k * P:(k + 1) * P], ident_h[:, :])
                mm.then_inc(q1_turned, 1)

            def rests(b, n, acc):
                r1 = [rest_part[:, c, 0:1].to_broadcast([P, P]) for c in range(3)]
                r2 = [rest_part[:, c, 1:2].to_broadcast([P, BANK]) for c in range(3)]
                for k in range(KT):
                    for c in range(3):
                        pe.matmul(acc[:, :], r1[c], q2[:, batch(b), k, cols(n)], start=False, stop=False)
                        pe.matmul(acc[:, :], q1T[:, b % 2, k, :], r2[c], start=False, stop=False)
                        for c2 in range(3):
                            pe.matmul(acc[:, :], r1[c], r2[c2], start=False, stop=False)

            def main(b, i, n):
                acc = ps_main[n % 2]
                if b == 1 and n < 2:
                    pe.wait_ge(x1_ready, n + 1)
                else:
                    wait(pe, x1_ready, b, i, NB, n - 1)
                if b == PER_B and n == 0:
                    pe.wait_ge(ctx2_coded, HALVES)
                for k in range(KT):
                    if n == 0 and k % HK == 0:
                        wait(pe, q1T_ready, b, i, 2, k // HK + 1)
                    if k == KT - 1:
                        with pe.If_ne(flag, 0):
                            rests(b, n, acc)
                    mm = pe.matmul(acc[:, :], q1T[:, b % 2, k, :], q2[:, batch(b), k, cols(n)],
                                   start=(k == 0), stop=(k == KT - 1))
                    if n == 3 and k == KT - 3:
                        turn_gate(b - 1, i)
                mm.then_inc(main_done, 1)

            def turn_h(b, i, h, src, ready, turned, free, per, extra):
                wait(pe, ready, b, i, 2, h + 1)
                wait(pe, free, b, i, per, extra)
                for k in range(HK):
                    mm = pe.transpose(as16(ps_turn[h], F16)[:, k * P:(k + 1) * P], src[:, h, k * P:(k + 1) * P], ident_h[:, :])
                mm.then_inc(turned, 1)

            def turn_hi(b, i, h):
                if b == TILES - 1:
                    turn_h(b, i, h, h_hi, h_hi_ready, hi_turned, loT_ready, 2, h - 1)
                    return
                turn_h(b, i, h, h_hi, h_hi_ready, hi_turned, q1T_ready, 2, 3 + h)

            def turn_lo(b, i, h):
                turn_h(b, i, h, h_lo, h_lo_ready, lo_turned, hiT_ready, 2, 1 + h)

            def mid_hi(b, i, h):
                wait(pe, hiT_ready, b, i, 2, h + 1)
                if h == 0:
                    wait(pe, mids_read, b, i, 1, 0)
                for k in range(HK):
                    kk = h * HK + k
                    if b == 0 and kk == 0:
                        pe.wait_ge(weights_split, 8)
                    mm = pe.matmul(ps_mid[:, 0:3 * J], hT[:, h, k, :], a_parts[:, kk, :, :].rearrange("p c j -> p (c j)"),
                                   start=(kk == 0), stop=False)
                mm.then_inc(hi_used, 1)

            def mid_lo(b, i, h):
                wait(pe, loT_ready, b, i, 2, h + 1)
                for k in range(HK):
                    kk = h * HK + k
                    mm = pe.matmul(ps_mid[:, J:3 * J], hT[:, h, k, :], a_parts[:, kk, 0:2, :].rearrange("p c j -> p (c j)"),
                                   start=False, stop=(kk == KT - 1))
                mm.then_inc(lo_used, 1)
                if h == 1:
                    mm_last = mm
                return mm

            def turn_gate(b, i):
                wait(pe, gated_ready, b, i, 1, 1)
                wait(pe, gT_ready, b, i, 1, 0)
                pe.transpose(ps_gate[:, 0:P], gated[:, :, :, :].rearrange("p d e r -> p (d e r)"),
                             ident_f[:, :]).then_inc(gate_turned, 1)

            def delta(b, i, n):
                acc = ps_delta[n % 2]
                wait(pe, gT_ready, b, i, 1, 1)
                wait(pe, out_ready, b, i, NB, n - 1)
                pe.matmul(acc[:, :], gT_hi[:, :], lora_bT[:, cols(n)], start=True, stop=False)
                pe.matmul(acc[:, :], gT_lo[:, :], lora_bT[:, cols(n)], start=False, stop=True).then_inc(delta_done, 1)

            turn_q1(0, 0, 0)
            turn_q1(0, 0, 1)
            def turn_weights(u):
                dst = ps_small[u % 2]
                if u >= 2:
                    pe.wait_ge(weights_split, u - 1)
                if u == 0:
                    pe.wait_ge(a_loaded, 32)
                for c in range(4):
                    if u < 4:
                        k = 4 * u + c
                        mm = pe.transpose(dst[:, c * J:(c + 1) * J], a_raw[0:J, k * P:(k + 1) * P], ident_f[0:J, 0:J])
                    else:
                        pe.wait_ge(b_spread, (u - 4) // 2 + 1)
                        mm = pe.transpose(dst[:, c * P:(c + 1) * P], b_flat[:, (4 * (u - 4) + c) % NC8, :], ident_f[:, :])
                mm.then_inc(weights_turned, 1)

            pe.wait_ge(q1T_ready, 2)
            for k in range(KT):
                pe.wait_ge(ctx_even, k + 1)
                pe.wait_ge(ctx_odd, k + 1)
                if k == KT - 1:
                    with pe.If_ne(flag, 0):
                        for n in range(NB):
                            rests(0, n, ps_first[n])
                for n in range(NB):
                    mm = pe.matmul(ps_first[n][:, :], q1T[:, 0, k, :], q2[:, 0, k, cols(n)],
                                   start=(k == 0), stop=(k == KT - 1))
                    if k == KT - 1:
                        mm.then_inc(main_done, 1)
                if k < 8:
                    turn_weights(k)
                if k in (9, 12):
                    turn_q1(1, 0, (k - 9) // 3)

            def slot(b, i):
                if b == 0:
                    return
                main(b, i, 0)
                if b >= 2:
                    delta(b - 2, i, 2)
                    delta(b - 2, i, 3)
                main(b, i, 1)
                if b >= 1:
                    turn_hi(b - 1, i, 0)
                    turn_hi(b - 1, i, 1)
                main(b, i, 2)
                if b >= 1:
                    mid_hi(b - 1, i, 0)
                    mid_hi(b - 1, i, 1)
                    turn_lo(b - 1, i, 0)
                    turn_lo(b - 1, i, 1)
                if b >= 1:
                    mid_lo(b - 1, i, 0)
                    mid_lo(b - 1, i, 1)
                if b < TILES - 1:
                    turn_q1(b + 1, i, 0)
                main(b, i, 3)
                if b < TILES - 1:
                    turn_q1(b + 1, i, 1)
                if b >= 1:
                    delta(b - 1, i, 0)
                    delta(b - 1, i, 1)

            slots(pe, slot)
            t = TILES - 1
            delta(t - 1, 0, 2)
            delta(t - 1, 0, 3)
            turn_hi(t, 0, 0)
            turn_hi(t, 0, 1)
            mid_hi(t, 0, 0)
            mid_hi(t, 0, 1)
            turn_lo(t, 0, 0)
            turn_lo(t, 0, 1)
            mid_lo(t, 0, 0)
            mid_lo(t, 0, 1)
            turn_gate(t, 0)
            for n in range(NB):
                delta(t, 0, n)

        GATE_STEPS = 9

        @block.vector
        def _(dve):
            dve.wait_ge(par_loaded, 96)
            nc.vector.reciprocal(inv_s[:, :], par[:, 0:2]).then_inc(par_step, 1)
            nc.vector.tensor_scalar(centre[:, :], par[:, 2:4], 0.0, QMAX, ALU.max, ALU.min).then_inc(par_step, 1)
            dve.wait_ge(par_step, 2)
            nc.vector.tensor_scalar(centre[:, :], centre[:, :], ROUND, -ROUND, ALU.add, ALU.add).then_inc(par_step, 1)
            dve.wait_ge(par_step, 3)
            nc.vector.tensor_scalar(neg_centre[:, :], centre[:, :], -1.0, -ROUND, ALU.mult, ALU.add).then_inc(par_step, 1)
            nc.vector.tensor_tensor(rest[:, :], centre[:, :], par[:, 2:4], ALU.subtract).then_inc(par_step, 1)
            dve.wait_ge(par_step, 5)
            nc.vector.tensor_copy(rest_part[:, 0, :], rest[:, :]).then_inc(par_step, 1)
            nc.vector.tensor_scalar(rest_flag[:, :], rest[:, :], 0.0, None, ALU.not_equal).then_inc(par_step, 1)
            dve.wait_ge(par_step, 7)
            nc.vector.tensor_tensor(rest_tmp[:, :], rest[:, :], rest_part[:, 0, :], ALU.subtract).then_inc(par_step, 1)
            nc.vector.tensor_reduce(rest_any[:, :], rest_flag[:, :], AX.X, ALU.max).then_inc(par_step, 1)
            dve.wait_ge(par_step, 9)
            nc.vector.tensor_copy(rest_part[:, 1, :], rest_tmp[:, :]).then_inc(par_step, 1)
            dve.wait_ge(par_step, 10)
            nc.vector.tensor_tensor(rest_part[:, 2, :], rest_tmp[:, :], rest_part[:, 1, :], ALU.subtract).then_inc(par_step, 1)
            dve.wait_ge(par_step, 11)
            dve.wait_ge(tanh_done, 1)
            nc.vector.tensor_scalar(gain[:, 0:1], gates_raw[:, 0:1], par[:, 0:1], par[:, 1:2], ALU.mult, ALU.mult).then_inc(par_step, 1)
            nc.vector.tensor_scalar(gain[:, 1:2], gates_raw[:, 1:2], LORA_SCALE, None, ALU.mult).then_inc(par_step, 1)
            dve.wait_ge(par_step, 13)
            nc.vector.memset(x_stats[:, :, :], 0.0).then_inc(consts_ready, 1)
            dve.wait_ge(consts_ready, 1)

            def split_a(g):
                src = ps_small[g % 2][:, 0:4 * J].rearrange("p (k j) -> p k j", j=J)
                tmp = h2[:, 0:4 * J].rearrange("p (k j) -> p k j", j=J)
                ks = slice(4 * g, 4 * g + 4)
                dve.wait_ge(weights_turned, g + 1)
                nc.vector.tensor_copy(a_parts[:, ks, 0, :], src).then_inc(a_step, 1)
                dve.wait_ge(a_step, 3 * g + 1)
                nc.vector.tensor_tensor(tmp, src, a_parts[:, ks, 0, :], ALU.subtract).then_inc(a_step, 1)
                dve.wait_ge(a_step, 3 * g + 2)
                nc.vector.tensor_copy(a_parts[:, ks, 1, :], tmp).then_inc(a_step, 1)
                dve.wait_ge(a_step, 3 * g + 3)
                nc.vector.tensor_tensor(a_parts[:, ks, 2, :], tmp, a_parts[:, ks, 1, :], ALU.subtract).then_inc(weights_split, 1)

            def spread_b(r):
                if r == 0:
                    dve.wait_ge(b_loaded, 16)
                else:
                    dve.wait_ge(weights_turned, 6)
                for d in range(2):
                    for e in range(E):
                        mv = nc.vector.tensor_copy(b_twice[:, :, d, e, :], b_raw[:, e, r * NC8:(r + 1) * NC8, :])
                mv.then_inc(b_spread, 1)

            def split_b(g):
                src = ps_small[g % 2][:, :].rearrange("q (c p) -> q c p", p=P)
                tmp = h2[:, 0:BANK].rearrange("q (c p) -> q c p", p=P)
                cs = slice(4 * g, 4 * g + 4)
                dve.wait_ge(weights_turned, g + 5)
                dve.wait_ge(weights_split, g + 4)
                nc.vector.tensor_copy(b_cols[0:ER, cs, :], src[0:ER]).then_inc(b_step, 1)
                nc.vector.tensor_copy(tmp[ER:P].bitcast(F32R), src[ER:P]).then_inc(b_step, 1)
                dve.wait_ge(b_step, 2 * g + 2)
                nc.vector.tensor_tensor(b_cols[ER:P, cs, :], src[ER:P], tmp[ER:P], ALU.subtract).then_inc(weights_split, 1)

            def round_ctx(b, i, q, extra):
                wait(dve, ctx_scaled, b, i, Q, extra)
                nc.vector.tensor_scalar(ctx_stage[:, q, :], ctx_stage[:, q, :], QMAX, ROUND, ALU.min, ALU.add).then_inc(ctx_rounded, 1)

            def code_ctx(batch_of, k, q, coded):
                nc.vector.tensor_scalar(q2[:, batch_of, k, half(q % 2)], ctx_stage[:, q, :], neg_centre[:, 1:2], None,
                                        ALU.add).then_inc(coded, 1)

            def stats_x(b, i):
                wait_half(dve, x_loaded[b % 2], b, i, 1)
                for n in range(NB):
                    nc.vector.bn_stats(x_stats[:, n, :], xt[:, b % 2, cols(n)]).then_inc(x_stat_step, 1)
                wait(dve, x_stat_step, b, i, NB + 1, NB)
                dve.sem_inc(dve_waited, 1)
                nc.vector.bn_aggr(x_mv[:, :], x_stats[:, :, :].rearrange("p n s -> p (n s)")).then_inc(x_stat_step, 1)
                wait(dve, x_stat_step, b, i, NB + 1, NB + 1)
                nc.vector.tensor_scalar(x_var[:, :], x_mv[:, 1:2], EPS, None, ALU.add).then_inc(x_var_ready, 1)

            def scale_of_x(b, i):
                wait(dve, x_rstd_ready, b, i, 1, 1)
                wait(dve, x_scaled, b, i, 2, 0)
                nc.vector.tensor_scalar(q_scale[:, 0:1], x_rstd[:, :], inv_s[:, 0:1], None, ALU.mult).then_inc(q_step, 1)
                nc.vector.tensor_scalar(q_neg[:, :], x_rstd[:, :], inv_s[:, 0:1], -1.0, ALU.mult, ALU.mult).then_inc(q_step, 1)
                wait(dve, q_step, b, i, 2, 2)
                nc.vector.tensor_scalar(q_scale[:, 1:2], x_mv[:, 0:1], q_neg[:, :], par[:, 2:3], ALU.mult, ALU.add).then_inc(q_scale_ready, 1)

            def round_x(b, i, h):
                wait(dve, x_scaled, b, i, 2, h + 1)
                nc.vector.tensor_scalar(w1[:, :], w1[:, :], QMAX, ROUND, ALU.min, ALU.add).then_inc(x_rounded, 1)

            def add_main(b, i, n):
                wait(dve, main_done, b, i, NB, n + 1)
                wait(dve, out_stored[n], b, i, 16, -16)
                nc.vector.scalar_tensor_tensor(out=x1[:, b % 2, cols(n)], in0=(ps_main[n % 2] if b else ps_first[n])[:, :], scalar=gain[:, 0:1],
                                               in1=xt[:, b % 2, cols(n)], op0=ALU.mult, op1=ALU.add).then_inc(x1_ready, 1)

            def stats_h(b, i, n):
                wait(dve, x1_ready, b, i, NB, n + 1)
                nc.vector.bn_stats(h_stats[:, n, :], x1[:, b % 2, cols(n)]).then_inc(h_stat_step, 1)

            def var_h(b, i):
                wait(dve, h_stat_step, b, i, NB + 1, NB)
                dve.sem_inc(dve_waited, 1)
                nc.vector.bn_aggr(h_mv[:, :], h_stats[:, :, :].rearrange("p n s -> p (n s)")).then_inc(h_stat_step, 1)
                wait(dve, h_stat_step, b, i, NB + 1, NB + 1)
                nc.vector.tensor_scalar(h_var[:, :], h_mv[:, 1:2], EPS, None, ALU.add).then_inc(h_var_ready, 1)

            def bias_h(b, i):
                wait(dve, h_rstd_ready, b, i, 1, 1)
                nc.vector.tensor_scalar(h_bias[:, :], h_mv[:, 0:1], h_rstd[:, :], -1.0, ALU.mult, ALU.mult).then_inc(h_bias_ready, 1)

            def copy_loT(b, i, h):
                wait(dve, lo_turned, b, i, 2, h + 1)
                wait(dve, hi_used, b, i, 2, h + 1)
                nc.vector.tensor_copy(hT[:, h, :, :],
                                      as16(ps_turn[h], F16).rearrange("p (k m) -> p k m", m=P)).then_inc(loT_ready, 1)

            def gating(b, i):
                def step(n):
                    wait(dve, gate_step, b, i, GATE_STEPS, n)
                wait(dve, lo_used, b, i, 2, 2)
                nc.vector.tensor_reduce(mids[:, :], ps_mid[:, 0:3 * J].rearrange("p (c j) -> p j c", j=J), AX.X,
                                        ALU.add).then_inc(mids_read, 1)
                wait(dve, mids_read, b, i, 1, 1)
                logits = mids[:, ER:J]
                each = logits.unsqueeze(1).to_broadcast([P, E, E])
                own = logits.unsqueeze(2).to_broadcast([P, E, E])
                nc.vector.tensor_reduce(top[:, :], logits, AX.X, ALU.max).then_inc(gate_step, 1)
                nc.vector.tensor_tensor(beats[:, :, 0, :], each, own, ALU.is_gt).then_inc(gate_step, 1)
                nc.vector.tensor_tensor(beats[:, :, 1, :], each, own, ALU.is_equal).then_inc(gate_step, 1)
                step(3)
                nc.vector.tensor_scalar(shifted[:, :], logits, top[:, :], None, ALU.subtract).then_inc(shifted_ready, 1)
                nc.vector.tensor_tensor(beats[:, :, 1, :], beats[:, :, 1, :], before[:, :, :], ALU.mult).then_inc(gate_step, 1)
                step(4)
                nc.vector.tensor_reduce(rank[:, :], beats[:, :, :, :].rearrange("p e c j -> p e (c j)"), AX.X,
                                        ALU.add).then_inc(gate_step, 1)
                step(5)
                wait(dve, exp_done, b, i, 1, 1)
                nc.vector.scalar_tensor_tensor(out=kept[:, :], in0=rank[:, :], scalar=1.5, in1=expd[:, :],
                                               op0=ALU.is_lt, op1=ALU.mult).then_inc(gate_step, 1)
                step(6)
                nc.vector.tensor_reduce(kept_sum[:, :], kept[:, :], AX.X, ALU.add).then_inc(gate_step, 1)
                step(7)
                nc.vector.reciprocal(kept_inv[:, :], kept_sum[:, :]).then_inc(gate_step, 1)
                step(8)
                nc.vector.tensor_scalar(gate[:, :], kept[:, :], kept_inv[:, :], gain[:, 1:2], ALU.mult, ALU.mult).then_inc(gate_step, 1)
                step(9)
                nc.vector.tensor_tensor(gated[:, :, :, :],
                                        mids[:, 0:ER].rearrange("p (e r) -> p e r", r=R).unsqueeze(1).to_broadcast([P, 2, E, R]),
                                        gate[:, :].unsqueeze(1).unsqueeze(3).to_broadcast([P, 2, E, R]), ALU.mult).then_inc(gated_ready, 1)

            def split_gate(b, i):
                wait(dve, gate_turned, b, i, 1, 1)
                wait(dve, delta_done, b, i, NB, 0)
                nc.vector.tensor_copy(gT_hi[:, :], ps_gate[:, 0:P]).then_inc(gT_step, 1)
                wait(dve, gT_step, b, i, 1, 1)
                nc.vector.tensor_tensor(gT_lo[:, :], ps_gate[:, 0:P], gT_hi[:, :].bitcast(F32), ALU.subtract).then_inc(gT_ready, 1)

            def add_delta(b, i, n):
                wait(dve, delta_done, b, i, NB, n + 1)
                nc.vector.tensor_tensor(x1[:, b % 2, cols(n)], ps_delta[n % 2][:, :], x1[:, b % 2, cols(n)],
                                        ALU.add).then_inc(out_ready, 1)

            stats_x(0, 0)
            scale_of_x(0, 0)
            for j in range(HALVES):
                round_ctx(0, 0, j % STAGES, j + 1)
                if j % 2 == 0:
                    dve.wait_ge(ctx_rounded, j + 1)
                    code_ctx(0, j // 2, j % STAGES, ctx_even)
                if j in (1, 4):
                    round_x(0, 0, j // 4)
                if j in (7, 9, 11, 13):
                    split_a((j - 7) // 2)
                if j == 12:
                    spread_b(0)
                if j in (14, 16):
                    split_b((j - 14) // 2)
                if j == 10:
                    stats_x(1, 0)
                if j == 16:
                    spread_b(1)
                    scale_of_x(1, 0)
                if j in (17, 20):
                    round_x(1, 0, (j - 17) // 3)
                if j in (19, 22):
                    split_b((j - 13) // 3)

            def slot(b, i):
                def ctx_half(q):
                    if b < PER_B:
                        k = (Q * b + q) // 2
                        round_ctx(b, i, q, HALVES + q + 1)
                        wait(dve, ctx_rounded, b, i, Q, HALVES + q + 1)
                        code_ctx(1, k if isinstance(i, int) else i * Q + k, q, ctx2_coded)
                ahead = 1 <= b < TILES - 1
                if b == 0:
                    ctx_half(0)
                    ctx_half(1)
                add_main(b, i, 0)
                stats_h(b, i, 0)
                if b >= 2:
                    add_delta(b - 2, i, 2)
                    add_delta(b - 2, i, 3)
                if ahead:
                    stats_x(b + 1, i)
                if b >= 1:
                    ctx_half(0)
                add_main(b, i, 1)
                stats_h(b, i, 1)
                if ahead:
                    scale_of_x(b + 1, i)
                if b >= 1:
                    ctx_half(1)
                if ahead:
                    round_x(b + 1, i, 0)
                add_main(b, i, 2)
                stats_h(b, i, 2)
                if ahead:
                    round_x(b + 1, i, 1)
                if b >= 1:
                    ctx_half(2)
                    copy_loT(b - 1, i, 0)
                    copy_loT(b - 1, i, 1)
                    ctx_half(3)
                    gating(b - 1, i)
                    split_gate(b - 1, i)
                add_main(b, i, 3)
                stats_h(b, i, 3)
                var_h(b, i)
                if b >= 1:
                    add_delta(b - 1, i, 0)
                bias_h(b, i)
                if b >= 1:
                    add_delta(b - 1, i, 1)
                if b == 0:
                    ctx_half(2)
                    ctx_half(3)

            slots(dve, slot)
            t = TILES - 1
            add_delta(t - 1, 0, 2)
            add_delta(t - 1, 0, 3)
            copy_loT(t, 0, 0)
            copy_loT(t, 0, 1)
            gating(t, 0)
            split_gate(t, 0)
            for n in range(NB):
                add_delta(t, 0, n)


_INS = ["x", "ctx_4096", "g_xattn", "g_ffn", "L0_xattn_x1_scale", "L0_xattn_x1_zp", "L0_xattn_x2_scale",
        "L0_xattn_x2_zp", "L0_ffn_A", "L0_ffn_B", "L0_ffn_Wr"]


def kernel(**inputs):
    import numpy as np
    import concourse.bacc as bacc
    from concourse.bass_utils import run_bass_kernel_spmd

    nc = bacc.Bacc("TRN2", target_bir_lowering=False, num_devices=1, dynamic_dma_scratch_size=128)
    arrays, args = {}, []
    for name in _INS:
        a = np.ascontiguousarray(inputs[name])
        arrays[f"in_{name}"] = a
        args.append(nc.dram_tensor(f"in_{name}", a.shape, mybir.dt.from_np(a.dtype), kind="ExternalInput").ap())
    shape = inputs["x"].shape
    out = nc.dram_tensor("out_x", shape, F32, kind="ExternalOutput").ap()
    build(nc, *args, out)
    r = run_bass_kernel_spmd(nc, [arrays], core_ids=[0])
    return r.results[0]["out_x"]
```

```python
from contextlib import ExitStack

import concourse.bass as bass
import concourse.mybir as mybir

ALU = mybir.AluOpType
ACT = mybir.ActivationFunctionType
AX = mybir.AxisListType
F32 = mybir.dt.float32
F32R = mybir.dt.float32r
BF16 = mybir.dt.bfloat16
F16 = mybir.dt.float16
I32 = mybir.dt.int32

P = 128
BANK = 512
HALF = 1024
ROUND = 1.5 * 2.0 ** 23
TURN = 0x6400
QMAX = 255.0
EPS = 1e-5
LORA_SCALE = 4.0
STAGES = 4


def build(nc, x, ctx_in, g_xattn, g_ffn, s1, z1, s2, z2, lora_a, lora_b, router, out):
    B, M, D = x.shape
    K, N = ctx_in.shape[1:]
    E, R, _ = lora_a.shape
    ER = E * R
    J = ER + E
    KT, NB = K // P, N // BANK
    TILES = B * M // P
    PER_B = M // P
    HALVES = 2 * KT
    Q = HALVES // PER_B
    ROWS = KT // 2
    CATCH = 10
    HK = HALF // P
    assert (D, N, Q, NB, 2 * ER) == (2 * HALF, D, STAGES, 4, P)

    x_rows = x.rearrange("b m d -> (b m) d")
    out_rows = out.rearrange("b m d -> (b m) d")
    ctx_rows = ctx_in.rearrange("b k n -> (b k) n")

    with ExitStack() as stack:
        def sb(name, shape, dt):
            return stack.enter_context(nc.sbuf_tensor(name, shape, dt))

        def sem(name):
            return stack.enter_context(nc.semaphore(name))

        q2 = sb("q2", [P, B, KT, N], F16)
        ctx_stage = sb("ctx_stage", [P, STAGES, HALF], F32)
        xt = sb("xt", [P, 2, D], F32)
        x1 = sb("x1", [P, 2, D], F32)
        q1T = sb("q1T", [P, 2, KT, P], F16)
        lora_bT = sb("lora_bT", [P, N], F32R)
        a_parts = sb("a_parts", [P, KT, 3, J], BF16)
        work = sb("work", [P, 2, HALF], F32)
        h_hi = sb("h_hi", [P, 2, HALF], F16)
        h_lo = sb("h_lo", [P, 2, HALF], F16)
        hT = sb("hT", [P, 2, HK, P], F16)
        ident_h = sb("ident_h", [P, P], F16)
        ident_f = sb("ident_f", [P, P], F32)
        small_tile = sb("small_tile", [P, 176], F32)
        used = [0]

        def small(*dims):
            n, first = 1, used[0]
            for d in dims:
                n *= d
            used[0] += n
            assert used[0] <= 176
            view = small_tile[:, first:first + n]
            if len(dims) == 2:
                return view.rearrange("p (a b) -> p a b", b=dims[1])
            if len(dims) == 3:
                return view.rearrange("p (a b c) -> p a b c", b=dims[1], c=dims[2])
            return view

        par = small(6)
        inv_s = small(2)
        centre = small(2)
        neg_centre = small(1)
        top_code = small(1)
        turn_bias = small(1)
        rest = small(2)
        rest_part = sb("rest_part", [P, 3, 2], BF16)
        rest_tmp = small(2)
        rest_flag = small(2)
        rest_any = sb("rest_any", [P, 1], I32)
        gates_raw = small(2)
        gain = small(2)
        round_col = small(1)
        half_neg = small(1)
        x_stats = small(NB, 6)
        x_mv = small(2)
        x_var = small(1)
        x_rstd = small(1)
        q_scale = small(2)
        q_neg = small(1)
        h_stats = small(NB, 6)
        h_mv = small(2)
        h_var = small(1)
        h_rstd = small(1)
        h_bias = small(1)
        before = small(E, E)
        mids = sb("mids", [P, J], F32)
        beats = small(E, 2, E)
        rank = small(E)
        top = small(1)
        shifted = small(E)
        expd = small(E)
        kept = small(E)
        kept_sum = small(1)
        kept_inv = small(1)
        gate = small(E)
        gated = sb("gated", [P, 2, E, R], F32)
        gT_hi = sb("gT_hi", [P, P], F32R)
        gT_lo = sb("gT_lo", [P, P], F32R)

        def bank(name):
            return stack.enter_context(nc.psum_tensor(name, [P, BANK], F32))

        ps_main = [bank("ps_main0"), bank("ps_main1")]
        ps_turn = [bank("ps_turn0"), bank("ps_turn1")]
        ps_mid = bank("ps_mid")
        ps_gate = bank("ps_gate")
        ps_delta = [bank("ps_delta0"), bank("ps_delta1")]
        ps_first = ps_main + ps_delta
        ps_small = [ps_mid, ps_gate]

        def product_bank(b, n):
            if b == 0:
                return ps_first[n]
            return ps_small[n] if b == 1 and n < 2 else ps_main[n % 2]


        par_loaded, a_loaded, b_loaded = sem("par_loaded"), sem("a_loaded"), sem("b_loaded")
        x_loaded = [[sem("x_loaded00"), sem("x_loaded01")], [sem("x_loaded10"), sem("x_loaded11")]]
        row_loaded = [sem(f"row_loaded{s}") for s in range(ROWS)]
        ctx_loaded = [sem(f"ctx_loaded{q}") for q in range(STAGES)]
        out_stored = [sem(f"out_stored{n}") for n in range(NB)]
        ident_zero, ident_ready, masks_ready = sem("ident_zero"), sem("ident_ready"), sem("masks_ready")
        par_step, consts_ready, tanh_done = sem("par_step"), sem("consts_ready"), sem("tanh_done")
        weights_turned, weights_split = sem("weights_turned"), sem("weights_split")
        a_step, b_spread, b_step = sem("a_step"), sem("b_spread"), sem("b_step")
        ctx_scaled = sem("ctx_scaled")
        left_rounded, late_rounded = sem("left_rounded"), sem("late_rounded")
        row_coded = sem("row_coded")
        ctx2_coded = sem("ctx2_coded")
        x_stat_step, x_var_ready, x_rstd_ready = sem("x_stat_step"), sem("x_var_ready"), sem("x_rstd_ready")
        q_step, q_scale_ready = sem("q_step"), sem("q_scale_ready")
        x_scaled, x_rounded = sem("x_scaled"), sem("x_rounded")
        row_scaled = sem("row_scaled")
        even_rounded, odd_rounded = sem("even_rounded"), sem("odd_rounded")
        q1_turned, q1T_ready = sem("q1_turned"), sem("q1T_ready")
        main_done, x1_ready = sem("main_done"), sem("x1_ready")
        h_stat_step, h_var_ready, h_rstd_ready = sem("h_stat_step"), sem("h_var_ready"), sem("h_rstd_ready")
        h_bias_ready = sem("h_bias_ready")
        h2_ready, h_hi_ready, h_lo_ready = sem("h2_ready"), sem("h_hi_ready"), sem("h_lo_ready")
        hi_turned, hiT_ready = sem("hi_turned"), sem("hiT_ready")
        lo_turned, loT_ready = sem("lo_turned"), sem("loT_ready")
        hi_used, lo_used, mid_done, mids_read = sem("hi_used"), sem("lo_used"), sem("mid_done"), sem("mids_read")
        gate_step, shifted_ready, exp_done = sem("gate_step"), sem("shifted_ready"), sem("exp_done")
        gated_ready, gate_turned, gT_step, gT_ready = sem("gated_ready"), sem("gate_turned"), sem("gT_step"), sem("gT_ready")
        pool_waited, dve_waited = sem("pool_waited"), sem("dve_waited")
        delta_done, out_ready = sem("delta_done"), sem("out_ready")

        block = stack.enter_context(nc.Block())

        def upto(b, i, per, extra):
            return per * b + extra + (i * (2 * per) if not isinstance(i, int) else 0)

        def wait(eng, s, b, i, per, extra):
            if isinstance(i, int) and per * b + extra <= 0:
                return
            eng.wait_ge(s, upto(b, i, per, extra))

        def wait_half(eng, s, b, i, n, unit=16):
            eng.wait_ge(s, unit * (b // 2 + n) + (i * unit if not isinstance(i, int) else 0))

        def slots(eng, body):
            for b in range(3):
                body(b, 0)
            with eng.Fori(0, (PER_B - 4) // 2) as i:
                body(3, i)
                body(4, i)
            body(PER_B - 1, 0)
            with eng.Fori(0, (PER_B - 2) // 2) as i:
                body(PER_B, i)
                body(PER_B + 1, i)
            body(TILES - 2, 0)
            body(TILES - 1, 0)

        def batch(b):
            return 0 if b < PER_B else 1

        def cols(n):
            return slice(n * BANK, (n + 1) * BANK)

        def half(h):
            return slice(h * HALF, (h + 1) * HALF)

        def as16(ps, dt):
            return ps[:, :].bitcast(dt)

        a_raw = x1[:, 0, :]
        b_raw = x1[:, 1, 0:HALF].rearrange("p (e c r) -> p e c r", e=E, r=R)
        b_twice = x1[:, 1, HALF:D].rearrange("p (c d e r) -> p c d e r", d=2, e=E, r=R)
        b_flat = x1[:, 1, HALF:D].rearrange("p (c j) -> p c j", j=P)
        row_stage = q2[:, 1, :, :].bitcast(F32).rearrange("p (s two) c -> p s (two c)", two=2)
        q1_bits = work[:, :, :].bitcast(F16).rearrange("p h (c two) -> p h c two", two=2)
        split_tmp = h_hi[:, 0, :].bitcast(F32)
        b_cols = lora_bT[:, :].rearrange("q (p c) -> q c p", c=KT)
        NC8 = HALF // P

        @block.sync
        def _(sp):
            def load_x(b, i, h):
                if b >= 2:
                    wait(sp, x1_ready, b, i, NB, 2 * h + 2 - 2 * NB)
                rows = bass.ts(b, P) if isinstance(i, int) else bass.ts(i * 2 + b, P)
                sp.dma_start(xt[:, b % 2, half(h)], x_rows[rows, half(h)]).then_inc(x_loaded[b % 2][h], 16)

            def load_ctx(row, h, q):
                sp.dma_start(ctx_stage[:, q, :], ctx_rows[row, half(h)]).then_inc(ctx_loaded[q], 16)

            load_x(0, 0, 0)
            load_x(0, 0, 1)
            for n, v in enumerate((s1, s2, z1, z2, g_xattn, g_ffn)):
                sp.dma_start(par[:, n:n + 1], v.unsqueeze(0).to_broadcast([P, 1])).then_inc(par_loaded, 16)
            for k in range(KT):
                if k >= ROWS:
                    sp.wait_ge(row_coded, k - ROWS + 1)
                sp.dma_start(row_stage[:, k % ROWS, :], ctx_rows[bass.ts(k, P), :]).then_inc(row_loaded[k % ROWS], 16)
                if k == 2:
                    sp.dma_start(a_raw[0:ER, :], lora_a.rearrange("e r f -> (e r) f")).then_inc(a_loaded, 16)
                    sp.dma_start(a_raw[ER:J, :], router).then_inc(a_loaded, 16)
                    sp.dma_start(x1[:, 1, 0:HALF].rearrange("p (e c) -> p e c", e=E),
                                 lora_b.rearrange("e (p c) r -> p e (c r)", c=KT)).then_inc(b_loaded, 16)
                if k == 3:
                    load_x(1, 0, 0)
                    load_x(1, 0, 1)
            for q in range(Q):
                load_ctx(bass.ts(KT + q // 2, P), q % 2, q)

            def slot(b, i):
                def ctx_half(q):
                    if b < PER_B - 1:
                        wait(sp, ctx2_coded, b, i, Q, q + 1)
                        row = (HALVES + Q * (b + 1) + q) // 2
                        rows = bass.ts(row, P) if isinstance(i, int) else bass.ts(i * Q + row, P)
                        load_ctx(rows, q % 2, q)
                if 1 <= b < TILES - 1:
                    load_x(b + 1, i, 1)
                ctx_half(0)
                if b >= 2:
                    store_out(b - 2, i, (2, 3))
                if b < TILES - 2:
                    load_x(b + 2, i, 0)
                ctx_half(1)
                ctx_half(2)
                ctx_half(3)
                if b >= 1:
                    store_out(b - 1, i, (0, 1))

            def store_out(b, i, banks):
                rows = bass.ts(b, P) if isinstance(i, int) else bass.ts(i * 2 + b, P)
                for n in banks:
                    wait(sp, out_ready, b, i, NB, n + 1)
                    sp.dma_start(out_rows[rows, cols(n)], x1[:, b % 2, cols(n)]).then_inc(out_stored[n], 16)

            slots(sp, slot)
            store_out(TILES - 2, 0, (2, 3))
            store_out(TILES - 1, 0, range(NB))
            for n in range(NB):
                sp.wait_ge(out_stored[n], 16 * TILES)

        @block.gpsimd
        def _(pool):
            nc.gpsimd.memset(ident_h[:, :], 0.0).then_inc(ident_zero, 1)
            nc.gpsimd.memset(ident_f[:, :], 0.0).then_inc(ident_zero, 1)
            nc.gpsimd.memset(before[:, :, :], 1.0).then_inc(ident_zero, 1)
            nc.gpsimd.memset(round_col[:, :], ROUND).then_inc(masks_ready, 1)
            nc.gpsimd.memset(half_neg[:, :], -0.5).then_inc(masks_ready, 1)
            pool.wait_ge(ident_zero, 3)
            for m in (ident_h, ident_f):
                nc.gpsimd.affine_select(out=m[:, :], in_=m[:, :], compare_op=ALU.not_equal, fill=1.0, base=0,
                                        pattern=[[-1, P]], channel_multiplier=1).then_inc(ident_ready, 1)
            nc.gpsimd.affine_select(out=before[:, :, :], in_=before[:, :, :], compare_op=ALU.is_gt, fill=0.0, base=0,
                                    pattern=[[1, E], [-1, E]], channel_multiplier=0).then_inc(masks_ready, 1)
            pool.wait_ge(masks_ready, 3)

            def power_x(b, i):
                wait(pool, x_var_ready, b, i, 1, 1)
                nc.gpsimd.tensor_tensor(x_rstd[:, :], x_var[:, :], half_neg[:, :], ALU.pow).then_inc(x_rstd_ready, 1)

            def power_h(b, i):
                wait(pool, h_var_ready, b, i, 1, 1)
                nc.gpsimd.tensor_tensor(h_rstd[:, :], h_var[:, :], half_neg[:, :], ALU.pow).then_inc(h_rstd_ready, 1)

            def low_part(b, i, h):
                wait(pool, h2_ready, b, i, 2, h + 1)
                wait(pool, h_hi_ready, b, i, 2, h + 1)
                wait(pool, lo_turned, b, i, 2, h - 1)
                nc.gpsimd.tensor_tensor(h_lo[:, h, :], work[:, h, :], h_hi[:, h, :], ALU.subtract).then_inc(h_lo_ready, 1)

            power_x(0, 0)
            pool.wait_ge(consts_ready, 3)
            for k in range(1, KT, 2):
                pool.wait_ge(row_scaled, k + 1)
                row = row_stage[:, k % ROWS, :]
                nc.gpsimd.tensor_scalar(row, row, ROUND, 1.0, ALU.add, ALU.mult).then_inc(odd_rounded, 1)
                if k == 3:
                    power_x(1, 0)

            def slot(b, i):
                if b >= 1:
                    low_part(b - 1, i, 0)
                if 1 <= b < TILES - 1:
                    power_x(b + 1, i)
                if b >= 1:
                    low_part(b - 1, i, 1)
                power_h(b, i)

            slots(pool, slot)
            for h in range(2):
                low_part(TILES - 1, 0, h)

        @block.scalar
        def _(act):
            act.wait_ge(par_loaded, 96)
            nc.scalar.activation(gates_raw[:, :], par[:, 4:6], ACT.Tanh).then_inc(tanh_done, 1)
            act.wait_ge(consts_ready, 3)
            act.wait_ge(masks_ready, 2)

            def scale_row(k):
                act.wait_ge(row_loaded[k % ROWS], 16 * (k // ROWS + 1))
                nc.scalar.activation(row_stage[:, k % ROWS, :], row_stage[:, k % ROWS, :], ACT.Relu,
                                     bias=par[:, 3:4], scale=inv_s[:, 1:2]).then_inc(row_scaled, 1)

            def scale_ctx(b, i, q):
                wait(act, ctx_loaded[q], b, i, 16, 16)
                nc.scalar.activation(ctx_stage[:, q, :], ctx_stage[:, q, :], ACT.Relu,
                                     bias=par[:, 3:4], scale=inv_s[:, 1:2]).then_inc(ctx_scaled, 1)

            def round_row(k):
                act.wait_ge(row_scaled, k + 1)
                nc.scalar.activation(row_stage[:, k % ROWS, :], row_stage[:, k % ROWS, :], ACT.Identity,
                                     bias=round_col[:, :], scale=1.0).then_inc(even_rounded, 1)

            def round_ctx(b, i, q):
                wait(act, ctx_scaled, b, i, Q, q + 1)
                nc.scalar.activation(ctx_stage[:, q, :], ctx_stage[:, q, :], ACT.Identity,
                                     bias=round_col[:, :], scale=1.0).then_inc(late_rounded, 1)

            def scale_x(b, i, h):
                wait(act, q_scale_ready, b, i, 1, 1)
                if b < 2:
                    wait(act, q1_turned, b, i, 2, h - 1)
                else:
                    wait(act, h_lo_ready, b, i, 2, h - 3)
                nc.scalar.activation(work[:, h, :], xt[:, b % 2, half(h)], ACT.Relu,
                                     bias=q_scale[:, 1:2], scale=q_scale[:, 0:1]).then_inc(x_scaled, 1)

            def copy_q1T(b, i, h):
                wait(act, q1_turned, b, i, 2, h + 1)
                nc.scalar.activation(q1T[:, b % 2, h * HK:(h + 1) * HK, :],
                                     as16(ps_turn[h], F16).rearrange("p (k m) -> p k m", m=P), ACT.Identity,
                                     bias=turn_bias[:, :], scale=1.0).then_inc(q1T_ready, 1)

            def high_part(b, i, h):
                wait(act, h_bias_ready, b, i, 1, 1)
                wait(act, hi_turned, b, i, 2, h - 1)
                nc.scalar.activation(h_hi[:, h, :], x1[:, b % 2, half(h)], ACT.Identity,
                                     bias=h_bias[:, :], scale=h_rstd[:, :]).then_inc(h_hi_ready, 1)

            def normal_half(b, i, h):
                if b < TILES - 1:
                    wait(act, q1_turned, b, i, 2, h + 3)
                nc.scalar.activation(work[:, h, :], x1[:, b % 2, half(h)], ACT.Identity,
                                     bias=h_bias[:, :], scale=h_rstd[:, :]).then_inc(h2_ready, 1)

            def copy_hiT(b, i, h):
                wait(act, hi_turned, b, i, 2, h + 1)
                wait(act, lo_used, b, i, 2, h - 1)
                nc.scalar.copy(hT[:, h, :, :],
                               as16(ps_turn[h], F16).rearrange("p (k m) -> p k m", m=P)).then_inc(hiT_ready, 1)

            def gate_exp(b, i):
                wait(act, shifted_ready, b, i, 1, 1)
                nc.scalar.activation(expd[:, :], shifted[:, :], ACT.Exp).then_inc(exp_done, 1)

            for k in range(KT):
                scale_row(k)
                if k == 0:
                    scale_x(0, 0, 0)
                    scale_x(0, 0, 1)
                if k % 2 == 0:
                    round_row(k)
                if k == 1:
                    copy_q1T(0, 0, 0)
                    copy_q1T(0, 0, 1)
                if k == 7:
                    scale_x(1, 0, 0)
                    scale_x(1, 0, 1)
                if k in (9, 10):
                    copy_q1T(1, 0, k - 9)

            def slot(b, i):
                def ctx_half(q):
                    if b < PER_B:
                        scale_ctx(b, i, q)
                ahead = 1 <= b < TILES - 1
                if b >= 1:
                    high_part(b - 1, i, 0)
                    normal_half(b - 1, i, 0)
                    high_part(b - 1, i, 1)
                ctx_half(0)
                if b >= 1:
                    normal_half(b - 1, i, 1)
                ctx_half(1)
                for h in range(2):
                    if b >= 1:
                        copy_hiT(b - 1, i, h)
                    if ahead:
                        scale_x(b + 1, i, h)
                ctx_half(2)
                if b < PER_B:
                    round_ctx(b, i, 2)
                ctx_half(3)
                if b < PER_B:
                    round_ctx(b, i, 3)
                if ahead:
                    copy_q1T(b + 1, i, 0)
                if b >= 1:
                    gate_exp(b - 1, i)
                if ahead:
                    copy_q1T(b + 1, i, 1)

            slots(act, slot)
            t = TILES - 1
            high_part(t, 0, 0)
            normal_half(t, 0, 0)
            high_part(t, 0, 1)
            normal_half(t, 0, 1)
            copy_hiT(t, 0, 0)
            copy_hiT(t, 0, 1)
            gate_exp(t, 0)

        @block.tensor
        def _(pe):
            flag = pe.alloc_register("rest_flag_reg")

            pe.wait_ge(consts_ready, 3)
            pe.reg_load(flag, rest_any[0:1, 0:1])

            def turn_q1(b, i, h):
                wait(pe, x_rounded, b, i, 2, h + 1)
                wait(pe, loT_ready, b, i, 2, h - 3)
                for k in range(HK):
                    mm = pe.transpose(as16(ps_turn[h], F16)[:, k * P:(k + 1) * P], q1_bits[:, h, k * P:(k + 1) * P, 0], ident_h[:, :])
                mm.then_inc(q1_turned, 1)

            def rests(b, n, acc):
                r1 = [rest_part[:, c, 0:1].to_broadcast([P, P]) for c in range(3)]
                r2 = [rest_part[:, c, 1:2].to_broadcast([P, BANK]) for c in range(3)]
                for k in range(KT):
                    for c in range(3):
                        pe.matmul(acc[:, :], r1[c], q2[:, batch(b), k, cols(n)], start=False, stop=False)
                        pe.matmul(acc[:, :], q1T[:, b % 2, k, :], r2[c], start=False, stop=False)
                        for c2 in range(3):
                            pe.matmul(acc[:, :], r1[c], r2[c2], start=False, stop=False)

            def main(b, i, n):
                acc = ps_main[n % 2]
                if b == 1:
                    pe.wait_ge(x1_ready, n - 1)
                else:
                    wait(pe, x1_ready, b, i, NB, n - 1)
                if b == PER_B and n == 0:
                    pe.wait_ge(ctx2_coded, HALVES)
                for k in range(KT):
                    if n == 0 and k % HK == 0:
                        wait(pe, q1T_ready, b, i, 2, k // HK + 1)
                    if k == KT - 1:
                        with pe.If_ne(flag, 0):
                            rests(b, n, acc)
                    mm = pe.matmul(acc[:, :], q1T[:, b % 2, k, :], q2[:, batch(b), k, cols(n)],
                                   start=(k == 0), stop=(k == KT - 1))
                    if n == 3 and k == KT - 3:
                        turn_gate(b - 1, i)
                mm.then_inc(main_done, 1)

            def turn_h(b, i, h, src, ready, turned, free, per, extra):
                wait(pe, ready, b, i, 2, h + 1)
                wait(pe, free, b, i, per, extra)
                for k in range(HK):
                    mm = pe.transpose(as16(ps_turn[h], F16)[:, k * P:(k + 1) * P], src[:, h, k * P:(k + 1) * P], ident_h[:, :])
                mm.then_inc(turned, 1)

            def turn_hi(b, i, h):
                if b == TILES - 1:
                    turn_h(b, i, h, h_hi, h_hi_ready, hi_turned, loT_ready, 2, h - 1)
                    return
                turn_h(b, i, h, h_hi, h_hi_ready, hi_turned, q1T_ready, 2, 3 + h)

            def turn_lo(b, i, h):
                turn_h(b, i, h, h_lo, h_lo_ready, lo_turned, hiT_ready, 2, 1 + h)

            def mid_hi(b, i, h):
                wait(pe, hiT_ready, b, i, 2, h + 1)
                if h == 0:
                    wait(pe, mids_read, b, i, 1, 0)
                for k in range(HK):
                    kk = h * HK + k
                    if b == 0 and kk == 0:
                        pe.wait_ge(x1_ready, NB + 1)
                    mm = pe.matmul(ps_mid[:, 0:3 * J], hT[:, h, k, :], a_parts[:, kk, :, :].rearrange("p c j -> p (c j)"),
                                   start=(kk == 0), stop=False)
                mm.then_inc(hi_used, 1)

            def mid_lo(b, i, h):
                wait(pe, loT_ready, b, i, 2, h + 1)
                for k in range(HK):
                    kk = h * HK + k
                    mm = pe.matmul(ps_mid[:, J:3 * J], hT[:, h, k, :], a_parts[:, kk, 0:2, :].rearrange("p c j -> p (c j)"),
                                   start=False, stop=(kk == KT - 1))
                mm.then_inc(lo_used, 1)

            def turn_gate(b, i):
                wait(pe, gated_ready, b, i, 1, 1)
                wait(pe, gT_ready, b, i, 1, 0)
                if b == 0:
                    pe.wait_ge(x1_ready, NB + 2)
                pe.transpose(ps_gate[:, 0:P], gated[:, :, :, :].rearrange("p d e r -> p (d e r)"),
                             ident_f[:, :]).then_inc(gate_turned, 1)

            def delta(b, i, n):
                acc = ps_delta[n % 2]
                wait(pe, gT_ready, b, i, 1, 1)
                wait(pe, out_ready, b, i, NB, n - 1)
                pe.matmul(acc[:, :], gT_hi[:, :], lora_bT[:, cols(n)], start=True, stop=False)
                pe.matmul(acc[:, :], gT_lo[:, :], lora_bT[:, cols(n)], start=False, stop=True).then_inc(delta_done, 1)

            turn_q1(0, 0, 0)
            turn_q1(0, 0, 1)
            def turn_weights(u):
                dst = ps_small[u % 2]
                if u >= 2:
                    pe.wait_ge(weights_split, u - 1)
                if u == 0:
                    pe.wait_ge(a_loaded, 32)
                for c in range(4):
                    if u < 4:
                        k = 4 * u + c
                        mm = pe.transpose(dst[:, c * J:(c + 1) * J], a_raw[0:J, k * P:(k + 1) * P], ident_f[0:J, 0:J])
                    else:
                        pe.wait_ge(b_spread, (u - 4) // 2 + 1)
                        mm = pe.transpose(dst[:, c * P:(c + 1) * P], b_flat[:, (4 * (u - 4) + c) % NC8, :], ident_f[:, :])
                mm.then_inc(weights_turned, 1)

            pe.wait_ge(q1T_ready, 2)
            for k in range(KT):
                pe.wait_ge(row_coded, k + 1)
                if k == KT - 1:
                    with pe.If_ne(flag, 0):
                        for n in range(NB):
                            rests(0, n, ps_first[n])
                for n in range(NB):
                    mm = pe.matmul(ps_first[n][:, :], q1T[:, 0, k, :], q2[:, 0, k, cols(n)],
                                   start=(k == 0), stop=(k == KT - 1))
                    if k == KT - 1:
                        mm.then_inc(main_done, 1)
                if 1 <= k <= 8:
                    turn_weights(k - 1)
                if k in (8, 9):
                    turn_q1(1, 0, k - 8)
                if k == CATCH:
                    pe.wait_ge(q1T_ready, 4)
                    pe.wait_ge(weights_split, 8)
                if k >= CATCH:
                    for kk in range(KT * (k - CATCH) // (KT - CATCH), KT * (k - CATCH + 1) // (KT - CATCH)):
                        if kk == KT - 1:
                            with pe.If_ne(flag, 0):
                                for n in range(2):
                                    rests(1, n, ps_small[n])
                        for n in range(2):
                            mm = pe.matmul(ps_small[n][:, :], q1T[:, 1, kk, :], q2[:, 0, kk, cols(n)],
                                           start=(kk == 0), stop=(kk == KT - 1))
                            if kk == KT - 1:
                                mm.then_inc(main_done, 1)

            def slot(b, i):
                if b == 0:
                    return
                if b >= 2:
                    main(b, i, 0)
                    delta(b - 2, i, 2)
                    delta(b - 2, i, 3)
                    main(b, i, 1)
                    turn_hi(b - 1, i, 0)
                    turn_hi(b - 1, i, 1)
                main(b, i, 2)
                if b == 1:
                    turn_hi(b - 1, i, 0)
                    turn_hi(b - 1, i, 1)
                for h in range(2):
                    mid_hi(b - 1, i, h)
                    turn_lo(b - 1, i, h)
                for h in range(2):
                    mid_lo(b - 1, i, h)
                if b < TILES - 1:
                    turn_q1(b + 1, i, 0)
                    turn_q1(b + 1, i, 1)
                main(b, i, 3)
                delta(b - 1, i, 0)
                delta(b - 1, i, 1)

            slots(pe, slot)
            t = TILES - 1
            delta(t - 1, 0, 2)
            delta(t - 1, 0, 3)
            turn_hi(t, 0, 0)
            turn_hi(t, 0, 1)
            mid_hi(t, 0, 0)
            mid_hi(t, 0, 1)
            turn_lo(t, 0, 0)
            turn_lo(t, 0, 1)
            mid_lo(t, 0, 0)
            mid_lo(t, 0, 1)
            turn_gate(t, 0)
            for n in range(NB):
                delta(t, 0, n)

        GATE_STEPS = 9

        @block.vector
        def _(dve):
            def parameters():
                dve.wait_ge(par_loaded, 96)
                nc.vector.reciprocal(inv_s[:, :], par[:, 0:2]).then_inc(par_step, 1)
                nc.vector.tensor_scalar(centre[:, :], par[:, 2:4], 0.0, QMAX, ALU.max, ALU.min).then_inc(par_step, 1)
                dve.wait_ge(par_step, 2)
                nc.vector.tensor_scalar(centre[:, :], centre[:, :], ROUND, -ROUND, ALU.add, ALU.add).then_inc(par_step, 1)
                dve.wait_ge(par_step, 3)
                nc.vector.tensor_scalar(neg_centre[:, :], centre[:, 1:2], -1.0, -ROUND, ALU.mult, ALU.add).then_inc(par_step, 1)
                nc.vector.tensor_scalar(top_code[:, :], centre[:, 1:2], -1.0, QMAX, ALU.mult, ALU.add).then_inc(consts_ready, 1)
                nc.vector.tensor_tensor(rest[:, :], centre[:, :], par[:, 2:4], ALU.subtract).then_inc(par_step, 1)
                dve.wait_ge(par_step, 5)
                nc.vector.tensor_scalar(turn_bias[:, :], centre[:, 0:1], -1.0, -1024.0, ALU.mult, ALU.add).then_inc(consts_ready, 1)
                nc.vector.tensor_copy(rest_part[:, 0, :], rest[:, :]).then_inc(par_step, 1)
                nc.vector.tensor_scalar(rest_flag[:, :], rest[:, :], 0.0, None, ALU.not_equal).then_inc(par_step, 1)
                dve.wait_ge(par_step, 7)
                nc.vector.tensor_tensor(rest_tmp[:, :], rest[:, :], rest_part[:, 0, :], ALU.subtract).then_inc(par_step, 1)
                nc.vector.tensor_reduce(rest_any[:, :], rest_flag[:, :], AX.X, ALU.max).then_inc(par_step, 1)
                dve.wait_ge(par_step, 9)
                nc.vector.tensor_copy(rest_part[:, 1, :], rest_tmp[:, :]).then_inc(par_step, 1)
                dve.wait_ge(par_step, 10)
                nc.vector.tensor_tensor(rest_part[:, 2, :], rest_tmp[:, :], rest_part[:, 1, :], ALU.subtract).then_inc(par_step, 1)
                dve.wait_ge(par_step, 11)
                dve.wait_ge(tanh_done, 1)
                nc.vector.tensor_scalar(gain[:, 0:1], gates_raw[:, 0:1], par[:, 0:1], par[:, 1:2], ALU.mult, ALU.mult).then_inc(par_step, 1)
                nc.vector.tensor_scalar(gain[:, 1:2], gates_raw[:, 1:2], LORA_SCALE, None, ALU.mult).then_inc(par_step, 1)
                dve.wait_ge(par_step, 13)
                dve.sem_inc(consts_ready, 1)

            def split_weights(u):
                if u < 4:
                    split_a(u)
                else:
                    split_b(u - 4)

            def split_a(g):
                src = ps_small[g % 2][:, 0:4 * J].rearrange("p (k j) -> p k j", j=J)
                tmp = split_tmp[:, 0:4 * J].rearrange("p (k j) -> p k j", j=J)
                ks = slice(4 * g, 4 * g + 4)
                dve.wait_ge(weights_turned, g + 1)
                nc.vector.tensor_copy(a_parts[:, ks, 0, :], src).then_inc(a_step, 1)
                dve.wait_ge(a_step, 3 * g + 1)
                nc.vector.tensor_tensor(tmp, src, a_parts[:, ks, 0, :], ALU.subtract).then_inc(a_step, 1)
                dve.wait_ge(a_step, 3 * g + 2)
                nc.vector.tensor_copy(a_parts[:, ks, 1, :], tmp).then_inc(a_step, 1)
                dve.wait_ge(a_step, 3 * g + 3)
                nc.vector.tensor_tensor(a_parts[:, ks, 2, :], tmp, a_parts[:, ks, 1, :], ALU.subtract).then_inc(weights_split, 1)

            def spread_b(r):
                if r == 0:
                    dve.wait_ge(b_loaded, 16)
                else:
                    dve.wait_ge(weights_turned, 6)
                for d in range(2):
                    for e in range(E):
                        mv = nc.vector.tensor_copy(b_twice[:, :, d, e, :], b_raw[:, e, r * NC8:(r + 1) * NC8, :])
                mv.then_inc(b_spread, 1)

            def split_b(g):
                src = ps_small[g % 2][:, :].rearrange("q (c p) -> q c p", p=P)
                tmp = split_tmp[:, 0:BANK].rearrange("q (c p) -> q c p", p=P)
                cs = slice(4 * g, 4 * g + 4)
                dve.wait_ge(weights_turned, g + 5)
                dve.wait_ge(weights_split, g + 4)
                nc.vector.tensor_copy(b_cols[0:ER, cs, :], src[0:ER]).then_inc(b_step, 1)
                nc.vector.tensor_copy(tmp[ER:P].bitcast(F32R), src[ER:P]).then_inc(b_step, 1)
                dve.wait_ge(b_step, 2 * g + 2)
                nc.vector.tensor_tensor(b_cols[ER:P, cs, :], src[ER:P], tmp[ER:P], ALU.subtract).then_inc(weights_split, 1)

            def clip_row(k):
                dve.wait_ge(odd_rounded if k % 2 else even_rounded, k // 2 + 1)
                nc.vector.tensor_scalar(q2[:, 0, k, :], row_stage[:, k % ROWS, :], neg_centre[:, :], top_code[:, :],
                                        ALU.add, ALU.min).then_inc(row_coded, 1)

            def stats_x(b, i, h):
                wait_half(dve, x_loaded[b % 2][h], b, i, 1)
                for n in (2 * h, 2 * h + 1):
                    nc.vector.bn_stats(x_stats[:, n, :], xt[:, b % 2, cols(n)]).then_inc(x_stat_step, 1)

            def var_x(b, i):
                wait(dve, x_stat_step, b, i, NB + 1, NB)
                dve.sem_inc(dve_waited, 1)
                nc.vector.bn_aggr(x_mv[:, :], x_stats[:, :, :].rearrange("p n s -> p (n s)")).then_inc(x_stat_step, 1)
                wait(dve, x_stat_step, b, i, NB + 1, NB + 1)
                nc.vector.tensor_scalar(x_var[:, :], x_mv[:, 1:2], EPS, None, ALU.add).then_inc(x_var_ready, 1)

            def scale_of_x(b, i):
                wait(dve, x_rstd_ready, b, i, 1, 1)
                wait(dve, x_scaled, b, i, 2, 0)
                nc.vector.tensor_scalar(q_scale[:, 0:1], x_rstd[:, :], inv_s[:, 0:1], None, ALU.mult).then_inc(q_step, 1)
                nc.vector.tensor_scalar(q_neg[:, :], x_rstd[:, :], inv_s[:, 0:1], -1.0, ALU.mult, ALU.mult).then_inc(q_step, 1)
                wait(dve, q_step, b, i, 2, 2)
                nc.vector.tensor_scalar(q_scale[:, 1:2], x_mv[:, 0:1], q_neg[:, :], par[:, 2:3], ALU.mult, ALU.add).then_inc(q_scale_ready, 1)

            def round_x(b, i, h):
                wait(dve, x_scaled, b, i, 2, h + 1)
                nc.vector.tensor_scalar(work[:, h, :], work[:, h, :], QMAX, ROUND + TURN, ALU.min, ALU.add).then_inc(x_rounded, 1)

            def add_main(b, i, n):
                wait(dve, main_done, b, i, NB, n + 1)
                wait(dve, out_stored[n], b, i, 16, -16)
                nc.vector.scalar_tensor_tensor(out=x1[:, b % 2, cols(n)], in0=product_bank(b, n)[:, :], scalar=gain[:, 0:1],
                                               in1=xt[:, b % 2, cols(n)], op0=ALU.mult, op1=ALU.add).then_inc(x1_ready, 1)

            def stats_h(b, i, n):
                wait(dve, x1_ready, b, i, NB, n + 1)
                nc.vector.bn_stats(h_stats[:, n, :], x1[:, b % 2, cols(n)]).then_inc(h_stat_step, 1)

            def var_h(b, i):
                wait(dve, h_stat_step, b, i, NB + 1, NB)
                dve.sem_inc(dve_waited, 1)
                nc.vector.bn_aggr(h_mv[:, :], h_stats[:, :, :].rearrange("p n s -> p (n s)")).then_inc(h_stat_step, 1)
                wait(dve, h_stat_step, b, i, NB + 1, NB + 1)
                nc.vector.tensor_scalar(h_var[:, :], h_mv[:, 1:2], EPS, None, ALU.add).then_inc(h_var_ready, 1)

            def bias_h(b, i):
                wait(dve, h_rstd_ready, b, i, 1, 1)
                nc.vector.tensor_scalar(h_bias[:, :], h_mv[:, 0:1], h_rstd[:, :], -1.0, ALU.mult, ALU.mult).then_inc(h_bias_ready, 1)

            def copy_loT(b, i, h):
                wait(dve, lo_turned, b, i, 2, h + 1)
                wait(dve, hi_used, b, i, 2, h + 1)
                nc.vector.tensor_copy(hT[:, h, :, :],
                                      as16(ps_turn[h], F16).rearrange("p (k m) -> p k m", m=P)).then_inc(loT_ready, 1)

            def step(b, i, n):
                wait(dve, gate_step, b, i, GATE_STEPS, n)

            def rank_gates(b, i):
                wait(dve, lo_used, b, i, 2, 2)
                nc.vector.tensor_reduce(mids[:, :], ps_mid[:, 0:3 * J].rearrange("p (c j) -> p j c", j=J), AX.X,
                                        ALU.add).then_inc(mids_read, 1)
                wait(dve, mids_read, b, i, 1, 1)
                logits = mids[:, ER:J]
                each = logits.unsqueeze(1).to_broadcast([P, E, E])
                own = logits.unsqueeze(2).to_broadcast([P, E, E])
                nc.vector.tensor_reduce(top[:, :], logits, AX.X, ALU.max).then_inc(gate_step, 1)
                nc.vector.tensor_tensor(beats[:, :, 0, :], each, own, ALU.is_gt).then_inc(gate_step, 1)
                nc.vector.tensor_tensor(beats[:, :, 1, :], each, own, ALU.is_equal).then_inc(gate_step, 1)
                step(b, i, 3)
                nc.vector.tensor_scalar(shifted[:, :], logits, top[:, :], None, ALU.subtract).then_inc(shifted_ready, 1)
                nc.vector.tensor_tensor(beats[:, :, 1, :], beats[:, :, 1, :], before[:, :, :], ALU.mult).then_inc(gate_step, 1)
                step(b, i, 4)
                nc.vector.tensor_reduce(rank[:, :], beats[:, :, :, :].rearrange("p e c j -> p e (c j)"), AX.X,
                                        ALU.add).then_inc(gate_step, 1)

            def weigh(b, i):
                step(b, i, 5)
                wait(dve, exp_done, b, i, 1, 1)
                nc.vector.scalar_tensor_tensor(out=kept[:, :], in0=rank[:, :], scalar=1.5, in1=expd[:, :],
                                               op0=ALU.is_lt, op1=ALU.mult).then_inc(gate_step, 1)
                step(b, i, 6)
                nc.vector.tensor_reduce(kept_sum[:, :], kept[:, :], AX.X, ALU.add).then_inc(gate_step, 1)
                step(b, i, 7)
                nc.vector.reciprocal(kept_inv[:, :], kept_sum[:, :]).then_inc(gate_step, 1)
                step(b, i, 8)
                nc.vector.tensor_scalar(gate[:, :], kept[:, :], kept_inv[:, :], gain[:, 1:2], ALU.mult, ALU.mult).then_inc(gate_step, 1)
                step(b, i, 9)
                nc.vector.tensor_tensor(gated[:, :, :, :],
                                        mids[:, 0:ER].rearrange("p (e r) -> p e r", r=R).unsqueeze(1).to_broadcast([P, 2, E, R]),
                                        gate[:, :].unsqueeze(1).unsqueeze(3).to_broadcast([P, 2, E, R]), ALU.mult).then_inc(gated_ready, 1)

            def split_gate(b, i):
                wait(dve, gate_turned, b, i, 1, 1)
                wait(dve, delta_done, b, i, NB, 0)
                nc.vector.tensor_copy(gT_hi[:, :], ps_gate[:, 0:P]).then_inc(gT_step, 1)
                wait(dve, gT_step, b, i, 1, 1)
                nc.vector.tensor_tensor(gT_lo[:, :], ps_gate[:, 0:P], gT_hi[:, :].bitcast(F32), ALU.subtract).then_inc(gT_ready, 1)

            def add_delta(b, i, n):
                wait(dve, delta_done, b, i, NB, n + 1)
                nc.vector.tensor_tensor(x1[:, b % 2, cols(n)], ps_delta[n % 2][:, :], x1[:, b % 2, cols(n)],
                                        ALU.add).then_inc(out_ready, 1)

            stats_x(0, 0, 0)
            stats_x(0, 0, 1)
            var_x(0, 0)
            parameters()
            scale_of_x(0, 0)
            for k in range(KT):
                if k == 0:
                    round_x(0, 0, 0)
                    round_x(0, 0, 1)
                clip_row(k)
                if k == 3:
                    spread_b(0)
                if k == 4:
                    stats_x(1, 0, 0)
                    stats_x(1, 0, 1)
                    var_x(1, 0)
                if k == 5:
                    scale_of_x(1, 0)
                if k == 7:
                    spread_b(1)
                if 2 <= k <= 9:
                    split_weights(k - 2)
                if k == 8:
                    round_x(1, 0, 0)
                    round_x(1, 0, 1)

            def slot(b, i):
                def round_half(q):
                    if b < PER_B:
                        wait(dve, ctx_scaled, b, i, Q, q + 1)
                        nc.vector.tensor_scalar(ctx_stage[:, q, :], ctx_stage[:, q, :], ROUND, None, ALU.add).then_inc(left_rounded, 1)

                def clip_half(q):
                    if b < PER_B:
                        k = (Q * b + q) // 2
                        wait(dve, left_rounded if q < 2 else late_rounded, b, i, 2, q % 2 + 1)
                        nc.vector.tensor_scalar(q2[:, 1, k if isinstance(i, int) else i * Q + k, half(q % 2)],
                                                ctx_stage[:, q, :], neg_centre[:, :], top_code[:, :], ALU.add, ALU.min).then_inc(ctx2_coded, 1)
                ahead = 1 <= b < TILES - 1
                add_main(b, i, 0)
                stats_h(b, i, 0)
                if ahead:
                    stats_x(b + 1, i, 1)
                    var_x(b + 1, i)
                if b >= 2:
                    add_delta(b - 2, i, 2)
                    add_delta(b - 2, i, 3)
                if ahead:
                    scale_of_x(b + 1, i)
                add_main(b, i, 1)
                stats_h(b, i, 1)
                round_half(0)
                round_half(1)
                clip_half(0)
                if ahead:
                    round_x(b + 1, i, 0)
                clip_half(1)
                add_main(b, i, 2)
                stats_h(b, i, 2)
                if b >= 1:
                    copy_loT(b - 1, i, 0)
                if ahead:
                    round_x(b + 1, i, 1)
                if b >= 1:
                    copy_loT(b - 1, i, 1)
                clip_half(2)
                if b >= 1:
                    rank_gates(b - 1, i)
                clip_half(3)
                if b >= 1:
                    weigh(b - 1, i)
                if b < TILES - 2:
                    stats_x(b + 2, i, 0)
                if b >= 1:
                    split_gate(b - 1, i)
                add_main(b, i, 3)
                stats_h(b, i, 3)
                var_h(b, i)
                if b >= 1:
                    add_delta(b - 1, i, 0)
                bias_h(b, i)
                if b >= 1:
                    add_delta(b - 1, i, 1)

            slots(dve, slot)
            t = TILES - 1
            add_delta(t - 1, 0, 2)
            add_delta(t - 1, 0, 3)
            copy_loT(t, 0, 0)
            copy_loT(t, 0, 1)
            rank_gates(t, 0)
            weigh(t, 0)
            split_gate(t, 0)
            for n in range(NB):
                add_delta(t, 0, n)


_INS = ["x", "ctx_4096", "g_xattn", "g_ffn", "L0_xattn_x1_scale", "L0_xattn_x1_zp", "L0_xattn_x2_scale",
        "L0_xattn_x2_zp", "L0_ffn_A", "L0_ffn_B", "L0_ffn_Wr"]


def kernel(**inputs):
    import numpy as np
    import concourse.bacc as bacc
    from concourse.bass_utils import run_bass_kernel_spmd

    nc = bacc.Bacc("TRN2", target_bir_lowering=False, num_devices=1, dynamic_dma_scratch_size=128)
    arrays, args = {}, []
    for name in _INS:
        a = np.ascontiguousarray(inputs[name])
        arrays[f"in_{name}"] = a
        args.append(nc.dram_tensor(f"in_{name}", a.shape, mybir.dt.from_np(a.dtype), kind="ExternalInput").ap())
    shape = inputs["x"].shape
    out = nc.dram_tensor("out_x", shape, F32, kind="ExternalOutput").ap()
    build(nc, *args, out)
    r = run_bass_kernel_spmd(nc, [arrays], core_ids=[0])
    return r.results[0]["out_x"]
```

```python
from contextlib import ExitStack

import concourse.bass as bass
import concourse.mybir as mybir

ALU = mybir.AluOpType
ACT = mybir.ActivationFunctionType
AX = mybir.AxisListType
F32 = mybir.dt.float32
F32R = mybir.dt.float32r
BF16 = mybir.dt.bfloat16
F16 = mybir.dt.float16
I32 = mybir.dt.int32

P = 128
BANK = 512
HALF = 1024
ROUND = 1.5 * 2.0 ** 23
TURN = 0x6400
QMAX = 255.0
EPS = 1e-5
LORA_SCALE = 4.0
STAGES = 4


def build(nc, x, ctx_in, g_xattn, g_ffn, s1, z1, s2, z2, lora_a, lora_b, router, out):
    B, M, D = x.shape
    K, N = ctx_in.shape[1:]
    E, R, _ = lora_a.shape
    ER = E * R
    J = ER + E
    KT, NB = K // P, N // BANK
    TILES = B * M // P
    PER_B = M // P
    HALVES = 2 * KT
    Q = HALVES // PER_B
    ROWS = KT // 2
    CATCH = 9
    HK = HALF // P
    assert (D, N, Q, NB, 2 * ER) == (2 * HALF, D, STAGES, 4, P)

    x_rows = x.rearrange("b m d -> (b m) d")
    out_rows = out.rearrange("b m d -> (b m) d")
    ctx_rows = ctx_in.rearrange("b k n -> (b k) n")

    with ExitStack() as stack:
        def sb(name, shape, dt):
            return stack.enter_context(nc.sbuf_tensor(name, shape, dt))

        def sem(name):
            return stack.enter_context(nc.semaphore(name))

        q2 = sb("q2", [P, B, KT, N], F16)
        ctx_stage = sb("ctx_stage", [P, STAGES, HALF], F32)
        xt = sb("xt", [P, 2, D], F32)
        x1 = sb("x1", [P, 2, D], F32)
        q1T = sb("q1T", [P, 2, KT, P], F16)
        lora_bT = sb("lora_bT", [P, N], F32R)
        a_parts = sb("a_parts", [P, KT, 3, J], BF16)
        work = sb("work", [P, 2, HALF], F32)
        h_hi = sb("h_hi", [P, 2, HALF], F16)
        h_lo = sb("h_lo", [P, 2, HALF], F16)
        hT = sb("hT", [P, 2, HK, P], F16)
        ident_h = sb("ident_h", [P, P], F16)
        ident_f = sb("ident_f", [P, P], F32)
        small_tile = sb("small_tile", [P, 176], F32)
        used = [0]

        def small(*dims):
            n, first = 1, used[0]
            for d in dims:
                n *= d
            used[0] += n
            assert used[0] <= 176
            view = small_tile[:, first:first + n]
            if len(dims) == 2:
                return view.rearrange("p (a b) -> p a b", b=dims[1])
            if len(dims) == 3:
                return view.rearrange("p (a b c) -> p a b c", b=dims[1], c=dims[2])
            return view

        par = small(6)
        inv_s = small(2)
        centre = small(2)
        neg_centre = small(1)
        top_code = small(1)
        turn_bias = small(1)
        rest = small(2)
        rest_part = sb("rest_part", [P, 3, 2], BF16)
        rest_tmp = small(2)
        rest_flag = small(2)
        rest_any = sb("rest_any", [P, 1], I32)
        gates_raw = small(2)
        gain = small(2)
        round_col = small(1)
        half_neg = small(1)
        x_stats = small(NB, 6)
        x_mv = small(2)
        x_var = small(1)
        x_rstd = small(1)
        q_scale = small(2)
        q_neg = small(1)
        h_stats = small(NB, 6)
        h_mv = small(2)
        h_var = small(1)
        h_rstd = small(1)
        h_bias = small(1)
        before = small(E, E)
        mids = sb("mids", [P, J], F32)
        beats = small(E, 2, E)
        rank = small(E)
        top = small(1)
        shifted = small(E)
        expd = small(E)
        kept = small(E)
        kept_sum = small(1)
        kept_inv = small(1)
        gate = small(E)
        gated = sb("gated", [P, 2, E, R], F32)
        gT_hi = sb("gT_hi", [P, P], F32R)
        gT_lo = sb("gT_lo", [P, P], F32R)

        def bank(name):
            return stack.enter_context(nc.psum_tensor(name, [P, BANK], F32))

        ps_main = [bank("ps_main0"), bank("ps_main1")]
        ps_turn = [bank("ps_turn0"), bank("ps_turn1")]
        ps_mid = bank("ps_mid")
        ps_gate = bank("ps_gate")
        ps_delta = [bank("ps_delta0"), bank("ps_delta1")]
        ps_first = ps_main + ps_delta
        ps_small = [ps_mid, ps_gate]

        def product_bank(b, n):
            if b == 0:
                return ps_first[n]
            return ps_small[n] if b == 1 and n < 2 else ps_main[n % 2]

        par_loaded, a_loaded, b_loaded = sem("par_loaded"), sem("a_loaded"), sem("b_loaded")
        x_loaded = [[sem("x_loaded00"), sem("x_loaded01")], [sem("x_loaded10"), sem("x_loaded11")]]
        row_loaded = [sem(f"row_loaded{s}") for s in range(ROWS)]
        ctx_loaded = [sem(f"ctx_loaded{q}") for q in range(STAGES)]
        out_stored = [sem(f"out_stored{n}") for n in range(NB)]
        ident_zero, ident_ready, masks_ready = sem("ident_zero"), sem("ident_ready"), sem("masks_ready")
        par_step, consts_ready, tanh_done = sem("par_step"), sem("consts_ready"), sem("tanh_done")
        weights_turned, weights_split = sem("weights_turned"), sem("weights_split")
        a_step, b_spread, b_step = sem("a_step"), sem("b_spread"), sem("b_step")
        ctx_scaled = sem("ctx_scaled")
        left_rounded, late_rounded = sem("left_rounded"), sem("late_rounded")
        row_coded = sem("row_coded")
        ctx2_coded = sem("ctx2_coded")
        x_stat_step, x_var_ready, x_rstd_ready = sem("x_stat_step"), sem("x_var_ready"), sem("x_rstd_ready")
        q_step, q_scale_ready = sem("q_step"), sem("q_scale_ready")
        x_scaled, x_rounded = sem("x_scaled"), sem("x_rounded")
        row_scaled = sem("row_scaled")
        fourth_rounded, others_rounded = sem("fourth_rounded"), sem("others_rounded")
        q1_turned, q1T_ready = sem("q1_turned"), sem("q1T_ready")
        main_done, x1_ready = sem("main_done"), sem("x1_ready")
        h_stat_step, h_var_ready, h_rstd_ready = sem("h_stat_step"), sem("h_var_ready"), sem("h_rstd_ready")
        h_bias_ready = sem("h_bias_ready")
        last_low_ready = sem("last_low_ready")
        h2_ready, h_hi_ready, h_lo_ready = sem("h2_ready"), sem("h_hi_ready"), sem("h_lo_ready")
        hi_turned, hiT_ready = sem("hi_turned"), sem("hiT_ready")
        lo_turned, loT_ready = sem("lo_turned"), [sem("loT_ready0"), sem("loT_ready1")]
        hi_used, lo_used, mids_read = sem("hi_used"), sem("lo_used"), sem("mids_read")
        gate_step, shifted_ready, exp_done = sem("gate_step"), sem("shifted_ready"), sem("exp_done")
        gated_ready, gate_turned, gT_step, gT_ready = sem("gated_ready"), sem("gate_turned"), sem("gT_step"), sem("gT_ready")
        dve_waited = sem("dve_waited")
        delta_done, out_ready = sem("delta_done"), sem("out_ready")

        block = stack.enter_context(nc.Block())

        def upto(b, i, per, extra):
            return per * b + extra + (i * (2 * per) if not isinstance(i, int) else 0)

        def wait(eng, s, b, i, per, extra):
            if isinstance(i, int) and per * b + extra <= 0:
                return
            eng.wait_ge(s, upto(b, i, per, extra))

        def wait_half(eng, s, b, i, n, unit=16):
            eng.wait_ge(s, unit * (b // 2 + n) + (i * unit if not isinstance(i, int) else 0))

        def slots(eng, body):
            for b in range(3):
                body(b, 0)
            with eng.Fori(0, (PER_B - 4) // 2) as i:
                body(3, i)
                body(4, i)
            body(PER_B - 1, 0)
            with eng.Fori(0, (PER_B - 2) // 2) as i:
                body(PER_B, i)
                body(PER_B + 1, i)
            body(TILES - 2, 0)
            body(TILES - 1, 0)

        def batch(b):
            return 0 if b < PER_B else 1

        def cols(n):
            return slice(n * BANK, (n + 1) * BANK)

        def half(h):
            return slice(h * HALF, (h + 1) * HALF)

        def as16(ps, dt):
            return ps[:, :].bitcast(dt)

        a_raw = x1[:, 0, :]
        b_raw = x1[:, 1, 0:HALF].rearrange("p (e c r) -> p e c r", e=E, r=R)
        b_twice = x1[:, 1, HALF:D].rearrange("p (c d e r) -> p c d e r", d=2, e=E, r=R)
        b_flat = x1[:, 1, HALF:D].rearrange("p (c j) -> p c j", j=P)
        row_stage = q2[:, 1, :, :].bitcast(F32).rearrange("p (s two) c -> p s (two c)", two=2)
        q1_bits = work[:, :, :].bitcast(F16).rearrange("p h (c two) -> p h c two", two=2)
        split_tmp = h_hi[:, 0, :].bitcast(F32)
        b_cols = lora_bT[:, :].rearrange("q (p c) -> q c p", c=KT)
        NC8 = HALF // P

        @block.sync
        def _(sp):
            def load_x(b, i, h):
                if b >= 2:
                    wait(sp, x1_ready, b, i, NB, 2 * h + 2 - 2 * NB)
                rows = bass.ts(b, P) if isinstance(i, int) else bass.ts(i * 2 + b, P)
                sp.dma_start(xt[:, b % 2, half(h)], x_rows[rows, half(h)]).then_inc(x_loaded[b % 2][h], 16)

            def load_ctx(row, h, q):
                sp.dma_start(ctx_stage[:, q, :], ctx_rows[row, half(h)]).then_inc(ctx_loaded[q], 16)

            load_x(0, 0, 0)
            load_x(0, 0, 1)
            for n, v in enumerate((s1, s2, z1, z2, g_xattn, g_ffn)):
                sp.dma_start(par[:, n:n + 1], v.unsqueeze(0).to_broadcast([P, 1])).then_inc(par_loaded, 16)
            for k in range(KT):
                if k >= ROWS:
                    sp.wait_ge(row_coded, k - ROWS + 1)
                sp.dma_start(row_stage[:, k % ROWS, :], ctx_rows[bass.ts(k, P), :]).then_inc(row_loaded[k % ROWS], 16)
                if k == 2:
                    sp.dma_start(a_raw[0:ER, :], lora_a.rearrange("e r f -> (e r) f")).then_inc(a_loaded, 16)
                    sp.dma_start(a_raw[ER:J, :], router).then_inc(a_loaded, 16)
                    sp.dma_start(x1[:, 1, 0:HALF].rearrange("p (e c) -> p e c", e=E),
                                 lora_b.rearrange("e (p c) r -> p e (c r)", c=KT)).then_inc(b_loaded, 16)
                if k == 3:
                    load_x(1, 0, 0)
                    load_x(1, 0, 1)
            for q in range(Q):
                load_ctx(bass.ts(KT + q // 2, P), q % 2, q)

            def slot(b, i):
                def ctx_half(q):
                    if b < PER_B - 1:
                        wait(sp, ctx2_coded, b, i, Q, q + 1)
                        row = (HALVES + Q * (b + 1) + q) // 2
                        rows = bass.ts(row, P) if isinstance(i, int) else bass.ts(i * Q + row, P)
                        load_ctx(rows, q % 2, q)
                if 3 <= b < TILES - 1:
                    load_x(b + 1, i, 1)
                if b >= 2:
                    store_out(b - 2, i, (2, 3))
                if b < TILES - 2:
                    load_x(b + 2, i, 0)
                if b == 0:
                    load_x(b + 2, i, 1)
                ctx_half(0)
                if b == 1:
                    load_x(b + 2, i, 1)
                    store_out(b - 1, i, (0, 1))
                ctx_half(1)
                ctx_half(2)
                ctx_half(3)
                if b >= 2:
                    store_out(b - 1, i, (0, 1))

            def store_out(b, i, banks):
                rows = bass.ts(b, P) if isinstance(i, int) else bass.ts(i * 2 + b, P)
                for n in banks:
                    wait(sp, out_ready, b, i, NB, n + 1)
                    sp.dma_start(out_rows[rows, cols(n)], x1[:, b % 2, cols(n)]).then_inc(out_stored[n], 16)

            slots(sp, slot)
            store_out(TILES - 2, 0, (2, 3))
            store_out(TILES - 1, 0, range(NB))
            for n in range(NB):
                sp.wait_ge(out_stored[n], 16 * TILES)

        @block.gpsimd
        def _(pool):
            nc.gpsimd.memset(ident_h[:, :], 0.0).then_inc(ident_zero, 1)
            nc.gpsimd.memset(ident_f[:, :], 0.0).then_inc(ident_zero, 1)
            nc.gpsimd.memset(before[:, :, :], 1.0).then_inc(ident_zero, 1)
            nc.gpsimd.memset(round_col[:, :], ROUND).then_inc(masks_ready, 1)
            nc.gpsimd.memset(half_neg[:, :], -0.5).then_inc(masks_ready, 1)
            pool.wait_ge(ident_zero, 3)
            for m in (ident_h, ident_f):
                nc.gpsimd.affine_select(out=m[:, :], in_=m[:, :], compare_op=ALU.not_equal, fill=1.0, base=0,
                                        pattern=[[-1, P]], channel_multiplier=1).then_inc(ident_ready, 1)
            nc.gpsimd.affine_select(out=before[:, :, :], in_=before[:, :, :], compare_op=ALU.is_gt, fill=0.0, base=0,
                                    pattern=[[1, E], [-1, E]], channel_multiplier=0).then_inc(masks_ready, 1)
            pool.wait_ge(masks_ready, 3)

            def power_x(b, i):
                wait(pool, x_var_ready, b, i, 1, 1)
                nc.gpsimd.tensor_tensor(x_rstd[:, :], x_var[:, :], half_neg[:, :], ALU.pow).then_inc(x_rstd_ready, 1)

            def power_h(b, i):
                wait(pool, h_var_ready, b, i, 1, 1)
                nc.gpsimd.tensor_tensor(h_rstd[:, :], h_var[:, :], half_neg[:, :], ALU.pow).then_inc(h_rstd_ready, 1)

            def low_part(b, i, h):
                wait(pool, h2_ready, b, i, 2, h + 1)
                wait(pool, h_hi_ready, b, i, 2, h + 1)
                wait(pool, lo_turned, b, i, 2, h - 1)
                nc.gpsimd.tensor_tensor(h_lo[:, h, :], work[:, h, :], h_hi[:, h, :], ALU.subtract).then_inc(h_lo_ready, 1)

            power_x(0, 0)
            pool.wait_ge(consts_ready, 3)
            for k in range(KT):
                if k % 4 == 0:
                    continue
                pool.wait_ge(row_scaled, k + 1)
                row = row_stage[:, k % ROWS, :]
                nc.gpsimd.tensor_scalar(row, row, ROUND, 1.0, ALU.add, ALU.mult).then_inc(others_rounded, 1)
                if k == 3:
                    power_x(1, 0)

            def slot(b, i):
                if b >= 1:
                    low_part(b - 1, i, 0)
                if 1 <= b < TILES - 1:
                    power_x(b + 1, i)
                if b >= 1:
                    low_part(b - 1, i, 1)
                power_h(b, i)

            slots(pool, slot)
            low_part(TILES - 1, 0, 0)

        @block.scalar
        def _(act):
            act.wait_ge(par_loaded, 96)
            nc.scalar.activation(gates_raw[:, :], par[:, 4:6], ACT.Tanh).then_inc(tanh_done, 1)
            act.wait_ge(consts_ready, 3)
            act.wait_ge(masks_ready, 3)

            def scale_row(k):
                act.wait_ge(row_loaded[k % ROWS], 16 * (k // ROWS + 1))
                nc.scalar.activation(row_stage[:, k % ROWS, :], row_stage[:, k % ROWS, :], ACT.Relu,
                                     bias=par[:, 3:4], scale=inv_s[:, 1:2]).then_inc(row_scaled, 1)

            def scale_ctx(b, i, q):
                wait(act, ctx_loaded[q], b, i, 16, 16)
                nc.scalar.activation(ctx_stage[:, q, :], ctx_stage[:, q, :], ACT.Relu,
                                     bias=par[:, 3:4], scale=inv_s[:, 1:2]).then_inc(ctx_scaled, 1)

            def round_ctx(b, i, q):
                wait(act, ctx_scaled, b, i, Q, q + 1)
                nc.scalar.activation(ctx_stage[:, q, :], ctx_stage[:, q, :], ACT.Identity,
                                     bias=round_col[:, :], scale=1.0).then_inc(late_rounded, 1)

            def scale_x(b, i, h):
                wait(act, q_scale_ready, b, i, 1, 1)
                if b < 2:
                    wait(act, q1_turned, b, i, 2, h - 1)
                else:
                    wait(act, h_lo_ready, b, i, 2, h - 3)
                nc.scalar.activation(work[:, h, :], xt[:, b % 2, half(h)], ACT.Relu,
                                     bias=q_scale[:, 1:2], scale=q_scale[:, 0:1]).then_inc(x_scaled, 1)

            def copy_q1T(b, i, h):
                wait(act, q1_turned, b, i, 2, h + 1)
                nc.scalar.activation(q1T[:, b % 2, h * HK:(h + 1) * HK, :],
                                     as16(ps_turn[h], F16).rearrange("p (k m) -> p k m", m=P), ACT.Identity,
                                     bias=turn_bias[:, :], scale=1.0).then_inc(q1T_ready, 1)

            def high_part(b, i, h):
                wait(act, h_bias_ready, b, i, 1, 1)
                wait(act, hi_turned, b, i, 2, h - 1)
                nc.scalar.activation(h_hi[:, h, :], x1[:, b % 2, half(h)], ACT.Identity,
                                     bias=h_bias[:, :], scale=h_rstd[:, :]).then_inc(h_hi_ready, 1)

            def normal_half(b, i, h):
                wait(act, q1_turned, b, i, 2, h + 3)
                nc.scalar.activation(work[:, h, :], x1[:, b % 2, half(h)], ACT.Identity,
                                     bias=h_bias[:, :], scale=h_rstd[:, :]).then_inc(h2_ready, 1)

            def copy_hiT(b, i, h):
                wait(act, hi_turned, b, i, 2, h + 1)
                wait(act, lo_used, b, i, 2, h - 1)
                nc.scalar.copy(hT[:, h, :, :],
                               as16(ps_turn[h], F16).rearrange("p (k m) -> p k m", m=P)).then_inc(hiT_ready, 1)

            def copy_loT(b, i):
                wait(act, lo_turned, b, i, 2, 1)
                wait(act, hi_used, b, i, 2, 1)
                nc.scalar.copy(hT[:, 0, :, :],
                               as16(ps_turn[0], F16).rearrange("p (k m) -> p k m", m=P)).then_inc(loT_ready[0], 1)

            def gate_exp(b, i):
                wait(act, shifted_ready, b, i, 1, 1)
                nc.scalar.activation(expd[:, :], shifted[:, :], ACT.Exp).then_inc(exp_done, 1)

            for k in range(KT):
                scale_row(k)
                if k == 0:
                    scale_x(0, 0, 0)
                    scale_x(0, 0, 1)
                if k == 1:
                    copy_q1T(0, 0, 0)
                    copy_q1T(0, 0, 1)
                if k == 5:
                    scale_x(1, 0, 0)
                    scale_x(1, 0, 1)
                if k in (8, 9):
                    copy_q1T(1, 0, k - 8)

            def slot(b, i):
                def scale(q):
                    if b < PER_B:
                        scale_ctx(b, i, q)

                def rounded(q):
                    if b < PER_B:
                        round_ctx(b, i, q)
                ahead = 1 <= b < TILES - 1
                if b == 0:
                    scale(1)
                    scale(2)
                    rounded(2)
                    scale(3)
                    rounded(3)
                    return
                for h in range(2):
                    high_part(b - 1, i, h)
                    normal_half(b - 1, i, h)
                if b == 1:
                    copy_hiT(b - 1, i, 0)
                    copy_hiT(b - 1, i, 1)
                    scale_x(b + 1, i, 0)
                    copy_loT(b - 1, i)
                    scale_x(b + 1, i, 1)
                    scale(0)
                    scale(1)
                    gate_exp(b - 1, i)
                    copy_q1T(b + 1, i, 0)
                    copy_q1T(b + 1, i, 1)
                    scale(2)
                    rounded(2)
                    scale(3)
                    rounded(3)
                    scale_ctx(b + 1, i, 0)
                    return
                scale(1)
                scale(2)
                copy_hiT(b - 1, i, 0)
                copy_hiT(b - 1, i, 1)
                if ahead:
                    scale_x(b + 1, i, 0)
                    scale_x(b + 1, i, 1)
                copy_loT(b - 1, i)
                rounded(2)
                scale(3)
                gate_exp(b - 1, i)
                rounded(3)
                if ahead:
                    copy_q1T(b + 1, i, 0)
                    copy_q1T(b + 1, i, 1)
                if b < PER_B - 1:
                    scale_ctx(b + 1, i, 0)

            scale_ctx(0, 0, 0)
            slots(act, slot)
            t = TILES - 1
            high_part(t, 0, 0)
            high_part(t, 0, 1)
            copy_hiT(t, 0, 0)
            copy_hiT(t, 0, 1)
            copy_loT(t, 0)
            gate_exp(t, 0)

        @block.tensor
        def _(pe):
            flag = pe.alloc_register("rest_flag_reg")

            pe.wait_ge(consts_ready, 3)
            pe.reg_load(flag, rest_any[0:1, 0:1])

            def turn_q1(b, i, h):
                wait(pe, x_rounded, b, i, 2, h + 1)
                wait(pe, loT_ready[h], b, i, 1, -1)
                for k in range(HK):
                    mm = pe.transpose(as16(ps_turn[h], F16)[:, k * P:(k + 1) * P], q1_bits[:, h, k * P:(k + 1) * P, 0], ident_h[:, :])
                mm.then_inc(q1_turned, 1)

            def rests(b, n, acc):
                r1 = [rest_part[:, c, 0:1].to_broadcast([P, P]) for c in range(3)]
                r2 = [rest_part[:, c, 1:2].to_broadcast([P, BANK]) for c in range(3)]
                for k in range(KT):
                    for c in range(3):
                        pe.matmul(acc[:, :], r1[c], q2[:, batch(b), k, cols(n)], start=False, stop=False)
                        pe.matmul(acc[:, :], q1T[:, b % 2, k, :], r2[c], start=False, stop=False)
                        for c2 in range(3):
                            pe.matmul(acc[:, :], r1[c], r2[c2], start=False, stop=False)

            def main(b, i, n):
                acc = ps_main[n % 2]
                if b == 1:
                    pe.wait_ge(x1_ready, n - 1)
                else:
                    wait(pe, x1_ready, b, i, NB, n - 1)
                if b == PER_B and n == 0:
                    pe.wait_ge(ctx2_coded, HALVES)
                for k in range(KT):
                    if n == 0 and k % HK == 0:
                        wait(pe, q1T_ready, b, i, 2, k // HK + 1)
                    if k == KT - 1:
                        with pe.If_ne(flag, 0):
                            rests(b, n, acc)
                    mm = pe.matmul(acc[:, :], q1T[:, b % 2, k, :], q2[:, batch(b), k, cols(n)],
                                   start=(k == 0), stop=(k == KT - 1))
                    if n == 3 and k == KT - 4:
                        turn_gate(b - 1, i)
                mm.then_inc(main_done, 1)

            def turn_h(b, i, h, src, ready, turned, free, per, extra):
                if ready is not None:
                    wait(pe, ready, b, i, 2, h + 1)
                wait(pe, free, b, i, per, extra)
                for k in range(HK):
                    mm = pe.transpose(as16(ps_turn[h], F16)[:, k * P:(k + 1) * P], src[:, h, k * P:(k + 1) * P], ident_h[:, :])
                mm.then_inc(turned, 1)

            def turn_hi(b, i, h):
                if b == TILES - 1:
                    turn_h(b, i, h, h_hi, h_hi_ready, hi_turned, loT_ready[h], 1, 0)
                    return
                turn_h(b, i, h, h_hi, h_hi_ready, hi_turned, q1T_ready, 2, 3 + h)

            def turn_lo(b, i, h):
                if (b, h) == (TILES - 1, 1):
                    pe.wait_ge(last_low_ready, 1)
                    turn_h(b, i, h, h_lo, None, lo_turned, hiT_ready, 2, 1 + h)
                    return
                turn_h(b, i, h, h_lo, h_lo_ready, lo_turned, hiT_ready, 2, 1 + h)

            def mid_hi(b, i, h):
                wait(pe, hiT_ready, b, i, 2, h + 1)
                if h == 0:
                    wait(pe, mids_read, b, i, 1, 0)
                for k in range(HK):
                    kk = h * HK + k
                    if b == 0 and kk == 0:
                        pe.wait_ge(x1_ready, NB + 1)
                    mm = pe.matmul(ps_mid[:, 0:3 * J], hT[:, h, k, :], a_parts[:, kk, :, :].rearrange("p c j -> p (c j)"),
                                   start=(kk == 0), stop=False)
                mm.then_inc(hi_used, 1)

            def mid_lo(b, i, h):
                wait(pe, loT_ready[h], b, i, 1, 1)
                for k in range(HK):
                    kk = h * HK + k
                    mm = pe.matmul(ps_mid[:, J:3 * J], hT[:, h, k, :], a_parts[:, kk, 0:2, :].rearrange("p c j -> p (c j)"),
                                   start=False, stop=(kk == KT - 1))
                mm.then_inc(lo_used, 1)

            def turn_gate(b, i):
                wait(pe, gated_ready, b, i, 1, 1)
                wait(pe, gT_ready, b, i, 1, 0)
                if b == 0:
                    pe.wait_ge(x1_ready, NB + 2)
                pe.transpose(ps_gate[:, 0:P], gated[:, :, :, :].rearrange("p d e r -> p (d e r)"),
                             ident_f[:, :]).then_inc(gate_turned, 1)

            def delta(b, i, first):
                wait(pe, gT_step, b, i, 1, 1)
                for n in (first, first + 1):
                    wait(pe, out_ready, b, i, NB, n - 1)
                    pe.matmul(ps_delta[n % 2][:, :], gT_hi[:, :], lora_bT[:, cols(n)], start=True, stop=False)
                wait(pe, gT_ready, b, i, 1, 1)
                for n in (first, first + 1):
                    pe.matmul(ps_delta[n % 2][:, :], gT_lo[:, :], lora_bT[:, cols(n)],
                              start=False, stop=True).then_inc(delta_done, 1)

            def turn_weights(u):
                dst = ps_small[u % 2]
                if u >= 2:
                    pe.wait_ge(weights_split, u - 1)
                if u == 0:
                    pe.wait_ge(a_loaded, 32)
                for c in range(4):
                    if u < 4:
                        k = 4 * u + c
                        mm = pe.transpose(dst[:, c * J:(c + 1) * J], a_raw[0:J, k * P:(k + 1) * P], ident_f[0:J, 0:J])
                    else:
                        pe.wait_ge(b_spread, (u - 4) // 2 + 1)
                        mm = pe.transpose(dst[:, c * P:(c + 1) * P], b_flat[:, (4 * (u - 4) + c) % NC8, :], ident_f[:, :])
                mm.then_inc(weights_turned, 1)

            pe.wait_ge(ident_ready, 2)
            turn_q1(0, 0, 0)
            turn_q1(0, 0, 1)

            pe.wait_ge(q1T_ready, 2)
            for k in range(KT):
                pe.wait_ge(row_coded, k + 1)
                if k == KT - 1:
                    with pe.If_ne(flag, 0):
                        for n in range(NB):
                            rests(0, n, ps_first[n])
                for n in range(NB):
                    mm = pe.matmul(ps_first[n][:, :], q1T[:, 0, k, :], q2[:, 0, k, cols(n)],
                                   start=(k == 0), stop=(k == KT - 1))
                    if k == KT - 1:
                        mm.then_inc(main_done, 1)
                if k < 8:
                    turn_weights(k)
                if k in (6, 7):
                    turn_q1(1, 0, k - 6)
                if k == CATCH:
                    pe.wait_ge(q1T_ready, 4)
                    pe.wait_ge(weights_split, 8)
                if k >= CATCH:
                    for kk in range(KT * (k - CATCH) // (KT - CATCH), KT * (k - CATCH + 1) // (KT - CATCH)):
                        if kk == KT - 1:
                            with pe.If_ne(flag, 0):
                                for n in range(2):
                                    rests(1, n, ps_small[n])
                        for n in range(2):
                            mm = pe.matmul(ps_small[n][:, :], q1T[:, 1, kk, :], q2[:, 0, kk, cols(n)],
                                           start=(kk == 0), stop=(kk == KT - 1))
                            if kk == KT - 1:
                                mm.then_inc(main_done, 1)

            def slot(b, i):
                if b == 0:
                    return
                if b >= 2:
                    main(b, i, 0)
                    delta(b - 2, i, 2)
                    main(b, i, 1)
                    turn_hi(b - 1, i, 0)
                    turn_hi(b - 1, i, 1)
                main(b, i, 2)
                if b == 1:
                    turn_hi(b - 1, i, 0)
                    turn_hi(b - 1, i, 1)
                for h in range(2):
                    mid_hi(b - 1, i, h)
                    turn_lo(b - 1, i, h)
                for h in range(2):
                    mid_lo(b - 1, i, h)
                    if b < TILES - 1:
                        turn_q1(b + 1, i, h)
                main(b, i, 3)
                delta(b - 1, i, 0)

            slots(pe, slot)
            t = TILES - 1
            delta(t - 1, 0, 2)
            turn_hi(t, 0, 0)
            turn_hi(t, 0, 1)
            for h in range(2):
                mid_hi(t, 0, h)
                turn_lo(t, 0, h)
            mid_lo(t, 0, 0)
            mid_lo(t, 0, 1)
            turn_gate(t, 0)
            delta(t, 0, 0)
            delta(t, 0, 2)

        GATE_STEPS = 9

        @block.vector
        def _(dve):
            def parameters():
                dve.wait_ge(par_loaded, 96)
                nc.vector.reciprocal(inv_s[:, :], par[:, 0:2]).then_inc(par_step, 1)
                nc.vector.tensor_scalar(centre[:, :], par[:, 2:4], 0.0, QMAX, ALU.max, ALU.min).then_inc(par_step, 1)
                dve.wait_ge(par_step, 2)
                nc.vector.tensor_scalar(centre[:, :], centre[:, :], ROUND, -ROUND, ALU.add, ALU.add).then_inc(par_step, 1)
                dve.wait_ge(par_step, 3)
                nc.vector.tensor_scalar(neg_centre[:, :], centre[:, 1:2], -1.0, -ROUND, ALU.mult, ALU.add).then_inc(par_step, 1)
                nc.vector.tensor_scalar(top_code[:, :], centre[:, 1:2], -1.0, QMAX, ALU.mult, ALU.add).then_inc(consts_ready, 1)
                nc.vector.tensor_tensor(rest[:, :], centre[:, :], par[:, 2:4], ALU.subtract).then_inc(par_step, 1)
                dve.wait_ge(par_step, 5)
                nc.vector.tensor_scalar(turn_bias[:, :], centre[:, 0:1], -1.0, -1024.0, ALU.mult, ALU.add).then_inc(consts_ready, 1)
                nc.vector.tensor_copy(rest_part[:, 0, :], rest[:, :]).then_inc(par_step, 1)
                nc.vector.tensor_scalar(rest_flag[:, :], rest[:, :], 0.0, None, ALU.not_equal).then_inc(par_step, 1)
                dve.wait_ge(par_step, 7)
                nc.vector.tensor_tensor(rest_tmp[:, :], rest[:, :], rest_part[:, 0, :], ALU.subtract).then_inc(par_step, 1)
                nc.vector.tensor_reduce(rest_any[:, :], rest_flag[:, :], AX.X, ALU.max).then_inc(par_step, 1)
                dve.wait_ge(par_step, 9)
                nc.vector.tensor_copy(rest_part[:, 1, :], rest_tmp[:, :]).then_inc(par_step, 1)
                dve.wait_ge(par_step, 10)
                nc.vector.tensor_tensor(rest_part[:, 2, :], rest_tmp[:, :], rest_part[:, 1, :], ALU.subtract).then_inc(par_step, 1)
                dve.wait_ge(par_step, 11)
                dve.wait_ge(tanh_done, 1)
                nc.vector.tensor_scalar(gain[:, 0:1], gates_raw[:, 0:1], par[:, 0:1], par[:, 1:2], ALU.mult, ALU.mult).then_inc(par_step, 1)
                nc.vector.tensor_scalar(gain[:, 1:2], gates_raw[:, 1:2], LORA_SCALE, None, ALU.mult).then_inc(par_step, 1)
                dve.wait_ge(par_step, 13)
                dve.sem_inc(consts_ready, 1)

            def split_weights(u):
                if u < 4:
                    split_a(u)
                else:
                    split_b(u - 4)

            def split_a(g):
                src = ps_small[g % 2][:, 0:4 * J].rearrange("p (k j) -> p k j", j=J)
                tmp = split_tmp[:, 0:4 * J].rearrange("p (k j) -> p k j", j=J)
                ks = slice(4 * g, 4 * g + 4)
                dve.wait_ge(weights_turned, g + 1)
                nc.vector.tensor_copy(a_parts[:, ks, 0, :], src).then_inc(a_step, 1)
                dve.wait_ge(a_step, 3 * g + 1)
                nc.vector.tensor_tensor(tmp, src, a_parts[:, ks, 0, :], ALU.subtract).then_inc(a_step, 1)
                dve.wait_ge(a_step, 3 * g + 2)
                nc.vector.tensor_copy(a_parts[:, ks, 1, :], tmp).then_inc(a_step, 1)
                dve.wait_ge(a_step, 3 * g + 3)
                nc.vector.tensor_tensor(a_parts[:, ks, 2, :], tmp, a_parts[:, ks, 1, :], ALU.subtract).then_inc(weights_split, 1)

            def spread_b(r):
                if r == 0:
                    dve.wait_ge(b_loaded, 16)
                else:
                    dve.wait_ge(weights_turned, 6)
                for d in range(2):
                    for e in range(E):
                        mv = nc.vector.tensor_copy(b_twice[:, :, d, e, :], b_raw[:, e, r * NC8:(r + 1) * NC8, :])
                mv.then_inc(b_spread, 1)

            def split_b(g):
                src = ps_small[g % 2][:, :].rearrange("q (c p) -> q c p", p=P)
                tmp = split_tmp[:, 0:BANK].rearrange("q (c p) -> q c p", p=P)
                cs = slice(4 * g, 4 * g + 4)
                dve.wait_ge(weights_turned, g + 5)
                dve.wait_ge(weights_split, g + 4)
                nc.vector.tensor_copy(b_cols[0:ER, cs, :], src[0:ER]).then_inc(b_step, 1)
                nc.vector.tensor_copy(tmp[ER:P].bitcast(F32R), src[ER:P]).then_inc(b_step, 1)
                dve.wait_ge(b_step, 2 * g + 2)
                nc.vector.tensor_tensor(b_cols[ER:P, cs, :], src[ER:P], tmp[ER:P], ALU.subtract).then_inc(weights_split, 1)

            def clip_row(k):
                row = row_stage[:, k % ROWS, :]
                if k % 4 == 0:
                    dve.wait_ge(row_scaled, k + 1)
                    nc.vector.tensor_scalar(row, row, ROUND, None, ALU.add).then_inc(fourth_rounded, 1)
                    dve.wait_ge(fourth_rounded, k // 4 + 1)
                else:
                    dve.wait_ge(others_rounded, k - k // 4)
                nc.vector.tensor_scalar(q2[:, 0, k, :], row, neg_centre[:, :], top_code[:, :],
                                        ALU.add, ALU.min).then_inc(row_coded, 1)

            def stats_x(b, i, h):
                wait_half(dve, x_loaded[b % 2][h], b, i, 1)
                for n in (2 * h, 2 * h + 1):
                    nc.vector.bn_stats(x_stats[:, n, :], xt[:, b % 2, cols(n)]).then_inc(x_stat_step, 1)

            def var_x(b, i):
                wait(dve, x_stat_step, b, i, NB + 1, NB)
                dve.sem_inc(dve_waited, 1)
                nc.vector.bn_aggr(x_mv[:, :], x_stats[:, :, :].rearrange("p n s -> p (n s)")).then_inc(x_stat_step, 1)
                wait(dve, x_stat_step, b, i, NB + 1, NB + 1)
                nc.vector.tensor_scalar(x_var[:, :], x_mv[:, 1:2], EPS, None, ALU.add).then_inc(x_var_ready, 1)

            def scale_of_x(b, i):
                wait(dve, x_rstd_ready, b, i, 1, 1)
                wait(dve, x_scaled, b, i, 2, 0)
                nc.vector.tensor_scalar(q_scale[:, 0:1], x_rstd[:, :], inv_s[:, 0:1], None, ALU.mult).then_inc(q_step, 1)
                nc.vector.tensor_scalar(q_neg[:, :], x_rstd[:, :], inv_s[:, 0:1], -1.0, ALU.mult, ALU.mult).then_inc(q_step, 1)
                wait(dve, q_step, b, i, 2, 2)
                nc.vector.tensor_scalar(q_scale[:, 1:2], x_mv[:, 0:1], q_neg[:, :], par[:, 2:3], ALU.mult, ALU.add).then_inc(q_scale_ready, 1)

            def round_x(b, i, h):
                wait(dve, x_scaled, b, i, 2, h + 1)
                nc.vector.tensor_scalar(work[:, h, :], work[:, h, :], QMAX, ROUND + TURN, ALU.min, ALU.add).then_inc(x_rounded, 1)

            def add_main(b, i, n):
                wait(dve, main_done, b, i, NB, n + 1)
                wait(dve, out_stored[n], b, i, 16, -16)
                nc.vector.scalar_tensor_tensor(out=x1[:, b % 2, cols(n)], in0=product_bank(b, n)[:, :], scalar=gain[:, 0:1],
                                               in1=xt[:, b % 2, cols(n)], op0=ALU.mult, op1=ALU.add).then_inc(x1_ready, 1)

            def stats_h(b, i, n):
                wait(dve, x1_ready, b, i, NB, n + 1)
                nc.vector.bn_stats(h_stats[:, n, :], x1[:, b % 2, cols(n)]).then_inc(h_stat_step, 1)

            def var_h(b, i):
                wait(dve, h_stat_step, b, i, NB + 1, NB)
                dve.sem_inc(dve_waited, 1)
                nc.vector.bn_aggr(h_mv[:, :], h_stats[:, :, :].rearrange("p n s -> p (n s)")).then_inc(h_stat_step, 1)
                wait(dve, h_stat_step, b, i, NB + 1, NB + 1)
                nc.vector.tensor_scalar(h_var[:, :], h_mv[:, 1:2], EPS, None, ALU.add).then_inc(h_var_ready, 1)

            def bias_h(b, i):
                wait(dve, h_rstd_ready, b, i, 1, 1)
                nc.vector.tensor_scalar(h_bias[:, :], h_mv[:, 0:1], h_rstd[:, :], -1.0, ALU.mult, ALU.mult).then_inc(h_bias_ready, 1)

            def copy_loT(b, i):
                wait(dve, lo_turned, b, i, 2, 2)
                wait(dve, hi_used, b, i, 2, 2)
                nc.vector.tensor_copy(hT[:, 1, :, :],
                                      as16(ps_turn[1], F16).rearrange("p (k m) -> p k m", m=P)).then_inc(loT_ready[1], 1)

            def step(b, i, n):
                wait(dve, gate_step, b, i, GATE_STEPS, n)

            def rank_gates(b, i):
                wait(dve, lo_used, b, i, 2, 2)
                nc.vector.tensor_reduce(mids[:, :], ps_mid[:, 0:3 * J].rearrange("p (c j) -> p j c", j=J), AX.X,
                                        ALU.add).then_inc(mids_read, 1)
                wait(dve, mids_read, b, i, 1, 1)
                logits = mids[:, ER:J]
                each = logits.unsqueeze(1).to_broadcast([P, E, E])
                own = logits.unsqueeze(2).to_broadcast([P, E, E])
                nc.vector.tensor_reduce(top[:, :], logits, AX.X, ALU.max).then_inc(gate_step, 1)
                nc.vector.tensor_tensor(beats[:, :, 0, :], each, own, ALU.is_gt).then_inc(gate_step, 1)
                nc.vector.tensor_tensor(beats[:, :, 1, :], each, own, ALU.is_equal).then_inc(gate_step, 1)
                step(b, i, 3)
                nc.vector.tensor_scalar(shifted[:, :], logits, top[:, :], None, ALU.subtract).then_inc(shifted_ready, 1)
                nc.vector.tensor_tensor(beats[:, :, 1, :], beats[:, :, 1, :], before[:, :, :], ALU.mult).then_inc(gate_step, 1)
                step(b, i, 4)
                nc.vector.tensor_reduce(rank[:, :], beats[:, :, :, :].rearrange("p e c j -> p e (c j)"), AX.X,
                                        ALU.add).then_inc(gate_step, 1)

            def weigh(b, i):
                step(b, i, 5)
                wait(dve, exp_done, b, i, 1, 1)
                nc.vector.scalar_tensor_tensor(out=kept[:, :], in0=rank[:, :], scalar=1.5, in1=expd[:, :],
                                               op0=ALU.is_lt, op1=ALU.mult).then_inc(gate_step, 1)
                step(b, i, 6)
                nc.vector.tensor_reduce(kept_sum[:, :], kept[:, :], AX.X, ALU.add).then_inc(gate_step, 1)
                step(b, i, 7)
                nc.vector.reciprocal(kept_inv[:, :], kept_sum[:, :]).then_inc(gate_step, 1)
                step(b, i, 8)
                nc.vector.tensor_scalar(gate[:, :], kept[:, :], kept_inv[:, :], gain[:, 1:2], ALU.mult, ALU.mult).then_inc(gate_step, 1)
                step(b, i, 9)
                nc.vector.tensor_tensor(gated[:, :, :, :],
                                        mids[:, 0:ER].rearrange("p (e r) -> p e r", r=R).unsqueeze(1).to_broadcast([P, 2, E, R]),
                                        gate[:, :].unsqueeze(1).unsqueeze(3).to_broadcast([P, 2, E, R]), ALU.mult).then_inc(gated_ready, 1)

            def split_gate(b, i):
                wait(dve, gate_turned, b, i, 1, 1)
                wait(dve, delta_done, b, i, NB, 0)
                nc.vector.tensor_copy(gT_hi[:, :], ps_gate[:, 0:P]).then_inc(gT_step, 1)
                wait(dve, gT_step, b, i, 1, 1)
                nc.vector.tensor_tensor(gT_lo[:, :], ps_gate[:, 0:P], gT_hi[:, :].bitcast(F32), ALU.subtract).then_inc(gT_ready, 1)

            def add_delta(b, i, n):
                wait(dve, delta_done, b, i, NB, n + 1)
                nc.vector.tensor_tensor(x1[:, b % 2, cols(n)], ps_delta[n % 2][:, :], x1[:, b % 2, cols(n)],
                                        ALU.add).then_inc(out_ready, 1)

            stats_x(0, 0, 0)
            stats_x(0, 0, 1)
            var_x(0, 0)
            parameters()
            scale_of_x(0, 0)
            for k in range(KT):
                if k == 0:
                    round_x(0, 0, 0)
                    round_x(0, 0, 1)
                clip_row(k)
                if k == 3:
                    spread_b(0)
                    stats_x(1, 0, 0)
                    stats_x(1, 0, 1)
                    var_x(1, 0)
                if k == 4:
                    scale_of_x(1, 0)
                if k == 5:
                    round_x(1, 0, 0)
                    round_x(1, 0, 1)
                if k == 6:
                    spread_b(1)
                if 1 <= k <= 8:
                    split_weights(k - 1)

            def slot(b, i):
                def round_half(q):
                    if b < PER_B:
                        wait(dve, ctx_scaled, b, i, Q, q + 1)
                        nc.vector.tensor_scalar(ctx_stage[:, q, :], ctx_stage[:, q, :], ROUND, None, ALU.add).then_inc(left_rounded, 1)

                def clip_half(q):
                    if b < PER_B:
                        k = (Q * b + q) // 2
                        wait(dve, left_rounded if q < 2 else late_rounded, b, i, 2, q % 2 + 1)
                        nc.vector.tensor_scalar(q2[:, 1, k if isinstance(i, int) else i * Q + k, half(q % 2)],
                                                ctx_stage[:, q, :], neg_centre[:, :], top_code[:, :], ALU.add, ALU.min).then_inc(ctx2_coded, 1)
                ahead = 1 <= b < TILES - 1
                if b == 0:
                    for n in range(NB):
                        add_main(b, i, n)
                        stats_h(b, i, n)
                    var_h(b, i)
                    round_half(0)
                    bias_h(b, i)
                    for n in range(2):
                        add_main(1, 0, n)
                        stats_h(1, 0, n)
                    round_half(1)
                    stats_x(b + 2, i, 0)
                    stats_x(b + 2, i, 1)
                    var_x(b + 2, i)
                    clip_half(0)
                    scale_of_x(b + 2, i)
                    for q in range(1, Q):
                        clip_half(q)
                    return
                if b == 1:
                    round_x(b + 1, i, 0)
                    add_main(b, i, 2)
                    stats_h(b, i, 2)
                    copy_loT(b - 1, i)
                    round_x(b + 1, i, 1)
                    rank_gates(b - 1, i)
                    round_half(0)
                    weigh(b - 1, i)
                    clip_half(0)
                    split_gate(b - 1, i)
                    add_main(b, i, 3)
                    stats_h(b, i, 3)
                    var_h(b, i)
                    add_delta(b - 1, i, 0)
                    bias_h(b, i)
                    add_delta(b - 1, i, 1)
                    round_half(1)
                    for q in range(1, Q):
                        clip_half(q)
                    return
                round_half(0)
                if ahead:
                    stats_x(b + 1, i, 0)
                add_main(b, i, 0)
                stats_h(b, i, 0)
                clip_half(0)
                if ahead:
                    stats_x(b + 1, i, 1)
                    var_x(b + 1, i)
                add_delta(b - 2, i, 2)
                add_delta(b - 2, i, 3)
                if ahead:
                    scale_of_x(b + 1, i)
                add_main(b, i, 1)
                stats_h(b, i, 1)
                if ahead:
                    round_x(b + 1, i, 0)
                add_main(b, i, 2)
                if ahead:
                    round_x(b + 1, i, 1)
                copy_loT(b - 1, i)
                stats_h(b, i, 2)
                round_half(1)
                rank_gates(b - 1, i)
                clip_half(1)
                weigh(b - 1, i)
                clip_half(2)
                split_gate(b - 1, i)
                clip_half(3)
                add_main(b, i, 3)
                stats_h(b, i, 3)
                var_h(b, i)
                add_delta(b - 1, i, 0)
                bias_h(b, i)
                add_delta(b - 1, i, 1)

            slots(dve, slot)
            t = TILES - 1
            dve.wait_ge(h_bias_ready, TILES)
            dve.wait_ge(h_lo_ready, 2 * t)
            for h in range(2):
                nc.vector.tensor_scalar(work[:, h, :], x1[:, t % 2, half(h)], h_rstd[:, :], h_bias[:, :],
                                        ALU.mult, ALU.add).then_inc(h2_ready, 1)
            dve.wait_ge(h2_ready, 2 * TILES)
            dve.wait_ge(h_hi_ready, 2 * TILES)
            dve.wait_ge(lo_turned, 2 * t)
            nc.vector.tensor_tensor(h_lo[:, 1, :], work[:, 1, :], h_hi[:, 1, :], ALU.subtract).then_inc(last_low_ready, 1)
            add_delta(t - 1, 0, 2)
            add_delta(t - 1, 0, 3)
            copy_loT(t, 0)
            rank_gates(t, 0)
            weigh(t, 0)
            split_gate(t, 0)
            for n in range(NB):
                add_delta(t, 0, n)


_INS = ["x", "ctx_4096", "g_xattn", "g_ffn", "L0_xattn_x1_scale", "L0_xattn_x1_zp", "L0_xattn_x2_scale",
        "L0_xattn_x2_zp", "L0_ffn_A", "L0_ffn_B", "L0_ffn_Wr"]


def kernel(**inputs):
    import numpy as np
    import concourse.bacc as bacc
    from concourse.bass_utils import run_bass_kernel_spmd

    nc = bacc.Bacc("TRN2", target_bir_lowering=False, num_devices=1, dynamic_dma_scratch_size=128)
    arrays, args = {}, []
    for name in _INS:
        a = np.ascontiguousarray(inputs[name])
        arrays[f"in_{name}"] = a
        args.append(nc.dram_tensor(f"in_{name}", a.shape, mybir.dt.from_np(a.dtype), kind="ExternalInput").ap())
    shape = inputs["x"].shape
    out = nc.dram_tensor("out_x", shape, F32, kind="ExternalOutput").ap()
    build(nc, *args, out)
    r = run_bass_kernel_spmd(nc, [arrays], core_ids=[0])
    return r.results[0]["out_x"]
```
